# Optimizing a Trainium2 kernel written in Bass

```python
import numpy as np
import jax
import jax.numpy as jnp

def _softmax(x, axis=-1):
    return jax.nn.softmax(x, axis=axis)

def _gelu(x):
    return jax.nn.gelu(x, approximate=True)

def _silu(x):
    return jax.nn.silu(x)

def _sigmoid(x):
    return jax.nn.sigmoid(x)

def _layernorm(x, axis=-1, eps=1e-05):
    m = jnp.mean(x, axis=axis, keepdims=True)
    v = jnp.var(x, axis=axis, keepdims=True)
    return (x - m) / jnp.sqrt(v + eps)

def _scatter_add(tgt, idx, src, axis=0):
    return tgt.at[idx].add(src)

def _segment_sum(src, seg, n):
    return jax.ops.segment_sum(src, seg, n)
kernel_name = 'mk_gnn_resnorm_d2_gnn_r8_a1c2d4'

def setup_inputs(seed: int=0):
    np.random.seed(seed)
    _w = jnp.asarray

    def _rec_inputs():
        import jax
        import jax.numpy as jnp
        _gk = jax.random.key(seed)
        x = -0.0003713 + 1 * jax.random.normal(jax.random.fold_in(_gk, 1), (6250, 128), jnp.float32)
        _s = jax.random.randint(jax.random.fold_in(_gk, 2), (50000,), 0, 6250, jnp.int32)
        _d = jax.random.randint(jax.random.fold_in(_gk, 3), (50000,), 0, 6250, jnp.int32)
        _loop = jnp.arange(6250, dtype=jnp.int32)
        src = jnp.concatenate([_s, _d, _loop])
        dst = jnp.concatenate([_d, _s, _loop])
        _o = jnp.argsort(dst, stable=True)
        src = src[_o]
        dst = dst[_o]
        edge_attr_128 = -4.21973e-05 + 0.999841 * jax.random.normal(jax.random.fold_in(_gk, 11), (106250, 128), jnp.float32)
        return (x, src, dst, edge_attr_128)
    x, src, dst, edge_attr_128 = _rec_inputs()

    def _L0_gnn_setup():
        import jax, jax.numpy as jnp
        import numpy as np
        BN_EPS = 1e-05
        key = jax.random.key(seed)
        k1, k2, k3, k4 = jax.random.split(key, 4)
        N, E, H, ED = (12500, 75000, 128, 128)
        node_feats = jax.random.normal(k1, (N, H), dtype=jnp.float32)
        edge_feats = jax.random.normal(k2, (E, ED), dtype=jnp.float32)
        W = jax.random.normal(k3, (2 * H, 2 * H + ED), dtype=jnp.float32) * 0.05
        b = jnp.zeros((2 * H,), dtype=jnp.float32)
        gamma = jnp.ones((2 * H,), dtype=jnp.float32)
        beta = jnp.zeros((2 * H,), dtype=jnp.float32)
        edge_index = jax.random.randint(k4, (2, E), 0, N, dtype=jnp.int64)
        return {'node_feats': node_feats, 'edge_feats': edge_feats, 'W': W, 'b': b, 'gamma': gamma, 'beta': beta, 'edge_index': edge_index}
    _L0_gnn_all = _L0_gnn_setup()
    _L0_gnn_in = {k: v for k, v in _L0_gnn_all.items() if k in ('W', 'b', 'gamma', 'beta')}
    del _L0_gnn_all

    def _L1_gnn_setup():
        import jax, jax.numpy as jnp
        import numpy as np
        ALPHA = 0.2
        LN_EPS = 1e-05
        key = jax.random.key(seed)
        ks = jax.random.split(key, 6)
        N, E, D = (12500, 75000, 128)
        x = jax.random.normal(ks[0], (N, D), dtype=jnp.float32)
        edge_index = jax.random.randint(ks[1], (2, E), 0, N, dtype=jnp.int64)
        W1 = jax.random.normal(ks[2], (D, D // 2), dtype=jnp.float32) * (1.0 / np.sqrt(D))
        b1 = jnp.zeros((D // 2,), dtype=jnp.float32)
        W2 = jax.random.normal(ks[3], (D // 2, D), dtype=jnp.float32) * (1.0 / np.sqrt(D // 2))
        b2 = jnp.zeros((D,), dtype=jnp.float32)
        gamma = jnp.ones((D,), dtype=jnp.float32)
        beta = jnp.zeros((D,), dtype=jnp.float32)
        return {'x': x, 'edge_index': edge_index, 'W1': W1, 'b1': b1, 'W2': W2, 'b2': b2, 'gamma': gamma, 'beta': beta}
    _L1_gnn_all = _L1_gnn_setup()
    _L1_gnn_in = {k: v for k, v in _L1_gnn_all.items() if k in ('W1', 'b1', 'W2', 'b2', 'gamma', 'beta')}
    del _L1_gnn_all
    return {'x': x, 'src': src, 'dst': dst, 'edge_attr_128': edge_attr_128, 'L0_gnn_W': _L0_gnn_in['W'], 'L0_gnn_b': _L0_gnn_in['b'], 'L0_gnn_gamma': _L0_gnn_in['gamma'], 'L0_gnn_beta': _L0_gnn_in['beta'], 'L1_gnn_W1': _L1_gnn_in['W1'], 'L1_gnn_b1': _L1_gnn_in['b1'], 'L1_gnn_W2': _L1_gnn_in['W2'], 'L1_gnn_b2': _L1_gnn_in['b2'], 'L1_gnn_gamma': _L1_gnn_in['gamma'], 'L1_gnn_beta': _L1_gnn_in['beta']}

def reference(x, src, dst, edge_attr_128, L0_gnn_W, L0_gnn_b, L0_gnn_gamma, L0_gnn_beta, L1_gnn_W1, L1_gnn_b1, L1_gnn_W2, L1_gnn_b2, L1_gnn_gamma, L1_gnn_beta):
    import jax
    import jax.numpy as jnp

    def _L0_gnn_ref(node_feats, edge_feats, W, b, gamma, beta, edge_index):
        import jax, jax.numpy as jnp
        import numpy as np
        BN_EPS = 1e-05
        H = node_feats.shape[1]
        src = edge_index[0]
        dst = edge_index[1]
        z = jnp.concatenate([node_feats[src], node_feats[dst], edge_feats], axis=1)
        z = z @ W.T + b
        mean = jnp.mean(z, axis=0)
        var = jnp.mean(jnp.square(z - mean), axis=0)
        z = (z - mean) * jax.lax.rsqrt(var + BN_EPS) * gamma + beta
        msg = jax.nn.sigmoid(z[:, :H]) * jax.nn.softplus(z[:, H:])
        agg = jnp.zeros_like(node_feats).at[src].add(msg)
        return node_feats + agg

    def _L1_gnn_ref(x, edge_index, W1, b1, W2, b2, gamma, beta):
        import jax, jax.numpy as jnp
        import numpy as np
        ALPHA = 0.2
        LN_EPS = 1e-05
        N = x.shape[0]
        src, dst = (edge_index[0], edge_index[1])
        msg_sum = jax.ops.segment_sum(x[src], dst, num_segments=N)
        cnt = jax.ops.segment_sum(jnp.ones_like(dst, dtype=x.dtype), dst, num_segments=N)
        local_mean = msg_sum / jnp.maximum(cnt, 1.0)[:, None]
        feature_diff = jnp.tanh(jnp.linalg.norm(x - local_mean, axis=1, keepdims=True))
        enhanced = jax.nn.relu(x @ W1 + b1) @ W2 + b2
        h = x + ALPHA * enhanced * feature_diff
        mu = jnp.mean(h, axis=-1, keepdims=True)
        var = jnp.var(h, axis=-1, keepdims=True)
        return (h - mu) * jax.lax.rsqrt(var + LN_EPS) * gamma + beta
    edge_index = jnp.stack([src, dst])
    x = _layernorm(x + _L0_gnn_ref(x, edge_attr_128, L0_gnn_W, L0_gnn_b, L0_gnn_gamma, L0_gnn_beta, edge_index), axis=-1)
    x = _layernorm(x + _L1_gnn_ref(x, edge_index, L1_gnn_W1, L1_gnn_b1, L1_gnn_W2, L1_gnn_b2, L1_gnn_gamma, L1_gnn_beta), axis=-1)
    return x

_drawn_inputs = setup_inputs


def setup_inputs(seed=0):
    import zlib

    import numpy as np

    out = dict(_drawn_inputs(seed))
    spreads = {'L0_gnn_b': (0.0, 0.8),
     'L0_gnn_gamma': (1.0, 0.2),
     'L0_gnn_beta': (0.0, 0.1),
     'L1_gnn_b1': (0.0, 0.8),
     'L1_gnn_b2': (0.0, 0.718),
     'L1_gnn_gamma': (1.0, 0.2),
     'L1_gnn_beta': (0.0, 0.1)}
    factors = {}
    for name, (base, spread) in spreads.items():
        noise = np.random.default_rng([zlib.crc32(name.encode()), seed]).standard_normal(out[name].shape)
        drawn = base * np.exp(spread * noise) if base else spread * noise
        out[name] = jnp.asarray(drawn.astype(out[name].dtype))
    for name, factor in factors.items():
        out[name] = (out[name] * factor).astype(out[name].dtype)
    return out
```

```python
from contextlib import ExitStack

import concourse.bass as bass
from concourse import mybir

ALU = mybir.AluOpType
ACT = mybir.ActivationFunctionType
AX_X = mybir.AxisListType.X
F32 = mybir.dt.float32
BF16 = mybir.dt.bfloat16
I32 = mybir.dt.int32
I16 = mybir.dt.int16
F16 = mybir.dt.float16
PE_ENGINE = mybir.EngineType.PE
DVE_ENGINE = mybir.EngineType.DVE

P = 128
N_NODES, N_EDGES, H = 6250, 106250, 128
Z = 2 * H
BLOCKS = -(-N_NODES // P)
ROWS = BLOCKS * P
LAST = N_NODES - (BLOCKS - 1) * P
T_IN = N_EDGES // P
TAIL = N_EDGES - P * T_IN
T_ALL = T_IN + 1
G_IN = 10
N_GROUPS_IN = T_IN // G_IN
G = 8
SLOTS = -(-((N_EDGES + BLOCKS * (P - 1)) // P) // (2 * G)) * (2 * G)
N_GROUPS = SLOTS // G
HALF = SLOTS // 2
REC = H + 2
BN_EPS = 1e-5
LN_EPS = 1e-5
ALPHA = 0.2
INVALID = 127 * P


def wait(eng, semaphore, value):
    if not isinstance(value, int) or value > 0:
        eng.wait_ge(semaphore, value)


def settle(eng, turns):
    eng.sem_inc(turns, 1)


def groups(eng, front, back, n, slots, lag=1):
    def turn(g, s, use):
        if not isinstance(g, int) or g < n:
            front(g, s, use)
        if back is not None and not (isinstance(g, int) and g < lag):
            back(g - lag, (s - lag) % slots, use if s >= lag else use - 1)

    for g in range(2 * slots):
        turn(g, g % slots, g // slots + 1)
    with eng.Fori(2, n // slots) as it:
        for s in range(slots):
            turn(slots * it + s, s, it + 1)
    if back is not None:
        for g in range(n, n + lag):
            turn(g, g % slots, g // slots + 1)


def build(nc, x, src, dst, edge, W, bias, gamma0, beta0, W1, b1, W2, b2, gamma1, beta1, out):
    ctx = ExitStack()
    with ctx:
        def sb(name, shape, dt):
            return ctx.enter_context(nc.sbuf_tensor(name, shape, dt))

        def sem(name):
            return ctx.enter_context(nc.semaphore(name))

        rec_d = nc.dram_tensor("rec_d", (P, SLOTS, REC), F32).ap()
        b_tab = nc.dram_tensor("b_tab", (ROWS, Z), F32).ap()
        z_d = nc.dram_tensor("z_d", (P, SLOTS, Z), F32).ap()
        x1_tab = nc.dram_tensor("x1_tab", (ROWS, H + 1), F32).ap()
        blk_d = nc.dram_tensor("blk_d", (2, P, 7), I32).ap()
        rec_rows = rec_d.rearrange("p t r -> (p t) r")

        x_sb = sb("x_sb", [P, BLOCKS, H], F32)
        ident = sb("ident", [P, P], F32)
        identb = sb("identb", [P, P], BF16)
        ones = sb("ones", [P, P], F32)
        tri = sb("tri", [P, P], F32)
        iota1 = sb("iota1", [P, P], F32)
        iota1b = sb("iota1b", [P, P], BF16)
        iota1h = sb("iota1h", [P, P], F16)
        iota_t = sb("iota_t", [P, SLOTS], F16)
        row0 = sb("row0", [P, P], F32)
        blk_row = sb("blk_row", [1, 2, P * 7], I32)
        srcloc = sb("srcloc", [P, SLOTS], F32)
        l1_loc = sb("l1_loc", [P, SLOTS], F32)
        l1_idx = sb("l1_idx", [P, SLOTS], I32)
        weT = sb("weT", [P, Z], F32)
        stat = sb("stat", [P, 16], F32)
        bn_s = stat[:, 0:2]
        bn_t = stat[:, 2:4]
        ARENA = 39000
        arena = sb("arena", [P, ARENA], F32)
        cursor = [0]

        def fresh(at=0):
            cursor[0] = at

        def tmp(shape, dt):
            n = 1
            for s in shape:
                n *= s
            words = n if dt in (F32, I32) else -(-n // 2)
            v = arena[:, cursor[0]:cursor[0] + words]
            cursor[0] += words
            assert cursor[0] <= ARENA, cursor[0]
            if dt != F32:
                v = v.bitcast(dt)
                if dt in (BF16, I16, F16):
                    v = v[:, 0:n]
            if len(shape) == 2:
                v = v.rearrange("p (a b) -> p a b", a=shape[0])
            elif len(shape) == 3:
                v = v.rearrange("p (a b c) -> p a b c", a=shape[0], b=shape[1])
            return v

        psum = ctx.enter_context(nc.psum_tensor("psum", [P, 8, 512], F32))

        def bank(i):
            return psum[:, i, :]

        src_i = tmp([T_ALL], I32)
        dst_i = tmp([T_ALL], I32)
        loc1 = tmp([T_ALL], F32)
        row_i = tmp([T_ALL], I32)
        lane_f = tmp([T_ALL], F32)
        tile_f = tmp([T_ALL], F32)
        v_a = tmp([T_ALL], F32)
        v_b = tmp([T_ALL], F32)
        EARLY = cursor[0]

        APARTS_AT = ARENA - BLOCKS * 3 * Z // 2
        aparts = arena[:, APARTS_AT:ARENA].bitcast(BF16).rearrange("p (b k z) -> p b k z", b=BLOCKS, k=3)

        def place_steps(tag, hi, pos, cnt, offs, h_ring, work, scalar_counts):
            s = {n: sem(f"{tag}_{n}") for n in
                 ("hot", "counted", "tot", "hot2", "scan", "pick", "chain", "blk", "blkd", "blkr")}
            tiles, tend, tstart, tcmp, blkf, blki, tnum = (
                work[n] for n in ("tiles", "tend", "tstart", "tcmp", "blkf", "blki", "tnum"))

            def vector(dve):
                def after(ins):
                    after.n += 1
                    ins.then_inc(s["chain"], 1)
                    dve.wait_ge(s["chain"], after.n)
                after.n = 0
                for b in range(BLOCKS):
                    if b >= 4:
                        dve.wait_ge(s["counted"], b - 3)
                    if scalar_counts:
                        nc.vector.tensor_scalar(h_ring[:, b % 4, :], hi, float(b), None, ALU.is_equal).then_inc(s["hot"], 1)
                    else:
                        nc.vector.tensor_scalar(h_ring[:, b % 4, :], hi, float(b), None, ALU.is_equal, ALU.add,
                                                accum_out=cnt[:, b:b + 1]).then_inc(s["counted"], 1)
                dve.wait_ge(s["tot"], 1)
                total, before = bank(7)[:, 0:BLOCKS], bank(7)[:, 64:64 + BLOCKS]
                after(nc.vector.tensor_scalar(tnum, total, 127.0, None, ALU.add))
                after(nc.vector.tensor_scalar(tnum, tnum, 7, None, ALU.logical_shift_right))
                after(nc.vector.tensor_copy(tiles, tnum))
                after(nc.vector.tensor_tensor_scan(tend, tiles, tiles, 0.0, ALU.add, ALU.bypass))
                after(nc.vector.tensor_tensor(tstart, tend, tiles, ALU.subtract))
                after(nc.vector.tensor_scalar(tstart, tstart, 128.0, -1.0, ALU.mult, ALU.add))
                after(nc.vector.tensor_tensor(offs, before, tstart, ALU.add))
                for c in range(7):
                    nc.vector.tensor_scalar(tcmp[:, c, :], tend, work["tile_id"][:, c:c + 1], None, ALU.is_le).then_inc(s["chain"], 1)
                after.n += 7
                dve.wait_ge(s["chain"], after.n)
                after(nc.vector.tensor_reduce(blkf, tcmp, op=ALU.add, axis=AX_X))
                after(nc.vector.tensor_scalar(blkf, blkf, float(BLOCKS - 1), None, ALU.min))
                nc.vector.tensor_copy(blki, blkf).then_inc(s["blk"], 1)
                nc.vector.memset(pos, 0.0).then_inc(s["pick"], 1)
                for b in range(BLOCKS):
                    if b >= 4:
                        dve.wait_ge(s["pick"], b - 2)
                    nc.vector.tensor_scalar(h_ring[:, b % 4, :], hi, float(b), None, ALU.is_equal).then_inc(s["hot2"], 1)
                    scan = psum[:, 2 * (b % 2):2 * (b % 2) + 2, :].rearrange("p a b -> p (a b)")[:, 0:T_ALL]
                    dve.wait_ge(s["hot2"], b + 1)
                    if b >= 2:
                        dve.wait_ge(s["pick"], b)
                    nc.vector.tensor_tensor_scan(scan, h_ring[:, b % 4, :], h_ring[:, b % 4, :], offs[:, b:b + 1],
                                                 ALU.add, ALU.bypass).then_inc(s["scan"], 1)
                    dve.wait_ge(s["scan"], b + 1)
                    dve.wait_ge(s["pick"], b + 1)
                    nc.vector.copy_predicated(pos, h_ring[:, b % 4, :].bitcast(I16), scan).then_inc(s["pick"], 1)
                dve.wait_ge(s["pick"], BLOCKS + 1)

            def scalar(act):
                for b in range(BLOCKS):
                    act.wait_ge(s["hot"], b + 1)
                    if b >= 2:
                        act.wait_ge(s["counted"], b - 1)
                    nc.scalar.activation(work["junk"][:, b % 2, :], h_ring[:, b % 4, :], ACT.Copy,
                                         accum_out=cnt[:, b:b + 1]).then_inc(s["counted"], 1)

            def tensor(pe):
                pe.wait_ge(s["counted"], BLOCKS)
                nc.tensor.matmul(bank(7)[:, 0:BLOCKS], ones[:], cnt, start=True, stop=True)
                nc.tensor.matmul(bank(7)[:, 64:64 + BLOCKS], tri[:], cnt, start=True, stop=True).then_inc(s["tot"], 1)

            def sync(sp, which):
                sp.wait_ge(s["blk"], 1)
                sp.dma_start(blk_d[which], blki).then_inc(s["blkd"], 16)
                sp.wait_ge(s["blkd"], 16)
                sp.dma_start(blk_row[0:1, which, :], blk_d[which:which + 1].rearrange("a p c -> a (p c)")).then_inc(s["blkr"], 16)
                sp.wait_ge(s["blkr"], 16)

            return vector, scalar, tensor, sync

        def place_work(junk):
            w = dict(tiles=tmp([BLOCKS], F32), tend=tmp([BLOCKS], F32), tstart=tmp([BLOCKS], F32),
                     tcmp=tmp([7, BLOCKS], F32), blkf=tmp([7], F32), blki=tmp([7], I32), tnum=tmp([BLOCKS], I32),
                     tile_id=tmp([7], F32))
            if junk:
                w["junk"] = tmp([2, T_ALL], BF16)
            return w

        fresh(EARLY)
        w_sb = tmp([2, 3 * H], F32)
        wabT = tmp([2 * Z], F32)
        bias_bc = tmp([Z], F32)
        xT = tmp([2, P], F32)
        a_f = tmp([4, Z], F32)
        b_f = tmp([4, Z], F32)
        hi = tmp([T_ALL], F32)
        hi_i = tmp([T_ALL], I32)
        pos = tmp([T_ALL], F32)
        pos_i = tmp([T_ALL], I32)
        h_ring = tmp([4, T_ALL + 1], BF16)[:, :, 0:T_ALL]
        cnt = tmp([BLOCKS], F32)
        offs = tmp([BLOCKS], F32)
        pwork = place_work(True)
        Z_RUN, Z_REP = 4, 20
        ZERO_TILES = Z_RUN * Z_REP
        zeros = tmp([Z_RUN * REC], F32)
        assert cursor[0] <= APARTS_AT, (cursor[0], APARTS_AT)

        s_const, s_ci, s_load, s_x, s_w = sem("const"), sem("const_int"), sem("ids_loaded"), sem("x_loaded"), sem("w_loaded")
        s_turn, s_sp_turn = sem("pool_turns"), sem("sync_turns")
        s_zero, s_zeroed, s_kc = sem("zeros_ready"), sem("rec_zeroed"), sem("key_chain")
        s_wt, s_we, s_xt, s_xe = sem("w_transposed"), sem("w_copied"), sem("x_transposed"), sem("x_copied")
        s_ab, s_ac, s_bc, s_am = sem("ab_product"), sem("a_copied"), sem("b_copied"), sem("a_middle")
        s_r1, s_sp = sem("a_rest"), sem("a_split")
        s_bst = [sem(f"b_stored{i}") for i in range(4)]
        pv, pa, pt, ps_ = place_steps("bysrc", hi, pos, cnt, offs, h_ring, pwork, True)
        N_CONST = 11

        with nc.Block() as block:
            @block.sync
            def _(sp):
                sp.wait_ge(s_ci, 3)
                for ids, col in ((src, src_i), (dst, dst_i)):
                    sp.dma_start(col[:, 0:T_IN], ids[0:P * T_IN].rearrange("(p t) -> p t", p=P)).then_inc(s_load, 16)
                    sp.dma_start(col[0:TAIL, T_IN:T_ALL], ids[P * T_IN:N_EDGES].rearrange("(p t) -> p t", t=1)).then_inc(s_load, 16)
                sp.dma_start(w_sb, W.rearrange("(h p) k -> p h k", p=P)).then_inc(s_w, 16)
                sp.dma_start(bias_bc, bias.rearrange("(a n) -> a n", a=1).broadcast_to([P, Z])).then_inc(s_w, 16)
                sp.dma_start(x_sb[:, 0:BLOCKS - 1, :], x[0:(BLOCKS - 1) * P, :].rearrange("(b p) f -> p b f", p=P)).then_inc(s_x, 16)
                sp.dma_start(x_sb[0:LAST, BLOCKS - 1, :], x[(BLOCKS - 1) * P:N_NODES, :]).then_inc(s_x, 16)
                sp.wait_ge(s_zero, 2)
                for c in range(SLOTS // ZERO_TILES):
                    sp.dma_start(rec_d[:, c * ZERO_TILES:(c + 1) * ZERO_TILES, :].rearrange("p (a t) r -> p a (t r)", a=Z_REP),
                                 zeros.unsqueeze(1).broadcast_to([P, Z_REP, Z_RUN * REC])).then_inc(s_zeroed, 16)
                ps_(sp, 0)
                sp.wait_ge(s_zeroed, 16 * (SLOTS // ZERO_TILES))

            @block.gpsimd
            def _(pool):
                nc.gpsimd.memset(src_i[:, T_IN:T_ALL], INVALID).then_inc(s_ci, 1)
                nc.gpsimd.memset(dst_i[:, T_IN:T_ALL], INVALID).then_inc(s_ci, 1)
                nc.gpsimd.memset(x_sb[:, BLOCKS - 1, :], 0.0).then_inc(s_ci, 1)
                nc.gpsimd.memset(zeros, 0.0).then_inc(s_zero, 1)
                nc.gpsimd.memset(ident[:], 0.0).then_inc(s_const, 1)
                nc.gpsimd.memset(ones[:], 1.0).then_inc(s_const, 1)
                pool.wait_ge(s_zero, 1)
                nc.gpsimd.memset(zeros.bitcast(I32).rearrange("p (t r) -> p t r", r=REC)[:, :, H:H + 1], N_NODES).then_inc(s_zero, 1)
                for ramp, first in ((iota1[:], 1), (iota1b[:], 1), (iota1h[:], 1), (iota_t[:], 0)):
                    nc.gpsimd.iota(ramp, [[1, ramp.shape[1]]], base=first, channel_multiplier=0,
                                   allow_small_or_imprecise_dtypes=True).then_inc(s_const, 1)
                nc.gpsimd.iota(pwork["tile_id"], [[1, 7]], base=0, channel_multiplier=7, allow_small_or_imprecise_dtypes=True).then_inc(s_const, 1)
                pool.wait_ge(s_const, 7)
                nc.gpsimd.affine_select(out=ident[:], in_=ident[:], compare_op=ALU.not_equal, fill=1.0, base=0,
                                        pattern=[[-1, P]], channel_multiplier=1).then_inc(s_const, 1)
                nc.gpsimd.affine_select(out=tri[:], in_=ones[:], compare_op=ALU.is_gt, fill=0.0, base=0,
                                        pattern=[[1, P]], channel_multiplier=-1).then_inc(s_const, 1)
                nc.gpsimd.affine_select(out=row0[:], in_=ones[:], compare_op=ALU.is_equal, fill=0.0, base=0,
                                        pattern=[[0, P]], channel_multiplier=1).then_inc(s_const, 1)
                pool.wait_ge(s_const, 10)
                nc.gpsimd.tensor_copy(identb[:], ident[:]).then_inc(s_const, 1)
                for b in range(BLOCKS + 1):
                    if b < BLOCKS:
                        a = a_f[:, b % 4, :]
                        pool.wait_ge(s_ac, 2 * b + 2)
                        nc.gpsimd.tensor_tensor(a, a, aparts[:, b, 0, :], ALU.subtract).then_inc(s_r1, 1)
                    if b >= 1:
                        pool.wait_ge(s_am, b)
                        nc.gpsimd.tensor_tensor(aparts[:, b - 1, 2, :], a_f[:, (b - 1) % 4, :], aparts[:, b - 1, 1, :],
                                                ALU.subtract).then_inc(s_sp, 1)

            @block.scalar
            def _(act):
                pa(act)
                act.wait_ge(s_wt, 1)
                nc.scalar.activation(wabT, bank(4), ACT.Copy).then_inc(s_we, 1)
                nc.scalar.activation(weT[:], bank(5)[:, 0:Z], ACT.Copy).then_inc(s_we, 1)

                def xt(b):
                    act.wait_ge(s_xt, b + 1)
                    if b >= 2:
                        act.wait_ge(s_ab, b - 1)
                    nc.scalar.activation(xT[:, b % 2, :], bank(6)[:, 0:P], ACT.Copy).then_inc(s_xe, 1)

                xt(0)
                for b in range(BLOCKS + 1):
                    if b + 1 < BLOCKS:
                        xt(b + 1)
                    if b < BLOCKS:
                        act.wait_ge(s_ab, b + 1)
                        nc.scalar.activation(aparts[:, b, 0, :], bank(4 + b % 2)[:, 0:Z], ACT.Copy).then_inc(s_ac, 1)
                        if b >= 4:
                            act.wait_ge(s_sp, b - 3)
                            act.wait_ge(s_bst[b % 4], 16 * (b // 4))
                        nc.scalar.activation(a_f[:, b % 4, :], bank(4 + b % 2)[:, 0:Z], ACT.Copy).then_inc(s_ac, 1)
                        nc.scalar.activation(b_f[:, b % 4, :], bank(4 + b % 2)[:, Z:2 * Z], ACT.Copy).then_inc(s_bc, 1)
                    if b >= 1:
                        act.wait_ge(s_r1, b)
                        nc.scalar.activation(aparts[:, b - 1, 1, :], a_f[:, (b - 1) % 4, :], ACT.Copy).then_inc(s_am, 1)
                        act.wait_ge(s_bc, b)
                        act.dma_start(b_tab[(b - 1) * P:b * P, :], b_f[:, (b - 1) % 4, :]).then_inc(s_bst[(b - 1) % 4], 16)
                for i in range(4):
                    act.wait_ge(s_bst[i], 16 * len(range(i, BLOCKS, 4)))

            @block.vector
            def _(dve):
                n = [0]

                def after(ins):
                    n[0] += 1
                    ins.then_inc(s_kc, 1)
                    dve.wait_ge(s_kc, n[0])

                dve.wait_ge(s_load, 64)
                after(nc.vector.tensor_scalar(hi_i, src_i, 7, None, ALU.logical_shift_right))
                after(nc.vector.tensor_copy(hi, hi_i))
                after(nc.vector.tensor_scalar(pos_i, src_i, P - 1, None, ALU.bitwise_and))
                dve.wait_ge(s_const, N_CONST)
                pv(dve)
                after(nc.vector.tensor_scalar(loc1, pos_i, 1.0, None, ALU.add))
                after(nc.vector.tensor_copy(pos_i, pos))
                after(nc.vector.tensor_scalar(hi_i, pos_i, P - 1, None, ALU.bitwise_and))
                after(nc.vector.tensor_scalar(pos_i, pos_i, 7, None, ALU.logical_shift_right))
                after(nc.vector.tensor_copy(hi, pos_i))
                after(nc.vector.scalar_tensor_tensor(pos, hi_i, float(SLOTS), hi, ALU.mult, ALU.add))
                after(nc.vector.tensor_copy(row_i, pos))

            @block.tensor
            def _(pe):
                pe.wait_ge(s_w, 32)
                pe.wait_ge(s_const, N_CONST)
                for h in range(2):
                    for part, dest in ((0, bank(4)[:, h * P:(h + 1) * P]), (1, bank(4)[:, Z + h * P:Z + (h + 1) * P]),
                                       (2, bank(5)[:, h * P:(h + 1) * P])):
                        last = nc.tensor.transpose(dest, w_sb[:, h, part * H:(part + 1) * H], ident[:])
                last.then_inc(s_wt, 1)
                pt(pe)
                pe.wait_ge(s_x, 32)
                pe.wait_ge(s_we, 2)

                def transpose(b):
                    if b >= 1:
                        pe.wait_ge(s_xe, b)
                    nc.tensor.transpose(bank(6)[:, 0:P], x_sb[:, b, :], ident[:]).then_inc(s_xt, 1)

                transpose(0)
                for b in range(BLOCKS):
                    if b + 1 < BLOCKS:
                        transpose(b + 1)
                    pe.wait_ge(s_xe, b + 1)
                    if b >= 2:
                        pe.wait_ge(s_bc, b - 1)
                    nc.tensor.matmul(bank(4 + b % 2), xT[:, b % 2, :], wabT, start=True, stop=False)
                    nc.tensor.matmul(bank(4 + b % 2)[:, 0:Z], row0[:], bias_bc, start=False, stop=True).then_inc(s_ab, 1)

        fresh(EARLY)
        e_buf = tmp([2, G_IN, REC], F32)
        e_idx = tmp([2, G_IN], I32)
        t_buf = tmp([REC], F32)
        hot_tile = tmp([2, SLOTS], F16)
        hot_lane = tmp([2, 2, P], F16)
        hi2 = tmp([T_ALL], F32)
        pos2 = tmp([T_ALL], F32)
        pos_i2 = tmp([T_ALL], I32)
        pos_j2 = tmp([T_ALL], I32)
        h_ring2 = tmp([4, T_ALL + 1], BF16)[:, :, 0:T_ALL]
        cnt2 = tmp([BLOCKS], F32)
        offs2 = tmp([BLOCKS], F32)
        pwork2 = place_work(False)
        l_a = tmp([SLOTS], F32)
        l_b = tmp([SLOTS], I32)
        l_c = tmp([SLOTS], I32)
        assert cursor[0] <= APARTS_AT, (cursor[0], APARTS_AT)
        s_kc2, s_const2 = sem("key_chain2"), sem("const2")
        pv2, _, pt2, ps2 = place_steps("bydst", hi2, pos2, cnt2, offs2, h_ring2, pwork2, False)
        s_el = [sem(f"edges_loaded{i}") for i in range(2)]
        s_er = [sem(f"rows_ready{i}") for i in range(2)]
        s_es = [sem(f"rows_scattered{i}") for i in range(2)]
        s_tl, s_tr, s_ts = sem("tail_loaded"), sem("tail_ready"), sem("tail_scattered")
        s_hot, s_list = sem("one_hots"), sem("list_product")
        edge_in = edge[0:P * T_IN, :].rearrange("(p t) f -> p t f", p=P)
        UL = 10
        assert T_IN % UL == 0 and N_NODES < ROWS

        with nc.Block() as block:
            @block.sync
            def _(sp):
                sp.dma_start(t_buf[0:TAIL, 0:H], edge[P * T_IN:N_EDGES, :]).then_inc(s_tl, 16)

                def load(g, s):
                    sp.dma_start(e_buf[:, s, :, 0:H], edge_in[:, bass.ds(g * G_IN, G_IN), :]).then_inc(s_el[s], 16)

                load(0, 0)
                load(1, 1)
                with sp.Fori(1, N_GROUPS_IN // 2) as it:
                    for s in range(2):
                        sp.wait_ge(s_es[s], it * (16 * G_IN))
                        settle(sp, s_sp_turn)
                        load(2 * it + s, s)
                sp.wait_ge(s_es[0], (N_GROUPS_IN // 2) * 16 * G_IN)
                load(N_GROUPS_IN - 1, 0)
                ps2(sp, 1)

            @block.scalar
            def _(act):
                def fill(g, s):
                    cols = bass.ds(g * G_IN, G_IN)
                    nc.scalar.activation(e_buf[:, s, :, H:H + 1].bitcast(I32).rearrange("p g a -> p (g a)"), dst_i[:, cols], ACT.Copy).then_inc(s_er[s], 1)
                    nc.scalar.activation(e_buf[:, s, :, H + 1:H + 2].rearrange("p g a -> p (g a)"), loc1[:, cols], ACT.Copy).then_inc(s_er[s], 1)
                    nc.scalar.activation(e_idx[:, s, :], row_i[:, cols], ACT.Copy).then_inc(s_er[s], 1)

                nc.scalar.activation(t_buf[:, H:H + 1].bitcast(I32), dst_i[:, T_IN:T_ALL], ACT.Copy).then_inc(s_tr, 1)
                nc.scalar.activation(t_buf[:, H + 1:H + 2], loc1[:, T_IN:T_ALL], ACT.Copy).then_inc(s_tr, 1)
                fill(0, 0)
                fill(1, 1)
                with act.Fori(1, N_GROUPS_IN // 2) as it:
                    for s in range(2):
                        act.wait_ge(s_es[s], it * (16 * G_IN))
                        fill(2 * it + s, s)
                act.wait_ge(s_es[0], (N_GROUPS_IN // 2) * 16 * G_IN)
                fill(N_GROUPS_IN - 1, 0)

            @block.gpsimd
            def _(pool):
                nc.gpsimd.iota(pwork2["tile_id"], [[1, 7]], base=0, channel_multiplier=7, allow_small_or_imprecise_dtypes=True).then_inc(s_const2, 1)

                def scatter(it1, s):
                    pool.wait_ge(s_el[s], it1 * 16)
                    pool.wait_ge(s_er[s], it1 * 3)
                    settle(pool, s_turn)
                    for k in range(G_IN):
                        nc.gpsimd.indirect_dma_start(rec_rows, bass.IndirectOffsetOnAxis(e_idx[:, s, k:k + 1], 0),
                                                     e_buf[:, s, k, :], None).then_inc(s_es[s], 16)

                pool.wait_ge(s_tl, 16)
                pool.wait_ge(s_tr, 2)
                nc.gpsimd.indirect_dma_start(rec_rows, bass.IndirectOffsetOnAxis(row_i[0:TAIL, T_IN:T_ALL], 0),
                                             t_buf[0:TAIL, :], None).then_inc(s_ts, 16)
                with pool.Fori(0, N_GROUPS_IN // 2) as it:
                    for s in range(2):
                        scatter(it + 1, s)
                scatter(N_GROUPS_IN // 2 + 1, 0)
                pool.wait_ge(s_es[0], (N_GROUPS_IN // 2 + 1) * 16 * G_IN)
                pool.wait_ge(s_es[1], (N_GROUPS_IN // 2) * 16 * G_IN)
                pool.wait_ge(s_ts, 16)

            @block.vector
            def _(dve):
                n = [0]

                def after(ins):
                    n[0] += 1
                    ins.then_inc(s_kc2, 1)
                    dve.wait_ge(s_kc2, n[0])

                after(nc.vector.tensor_scalar(pos_i2, dst_i, 7, None, ALU.logical_shift_right))
                after(nc.vector.tensor_copy(hi2, pos_i2))
                dve.wait_ge(s_const2, 1)
                pv2(dve)
                after(nc.vector.tensor_copy(pos_i2, pos2))
                after(nc.vector.tensor_scalar(pos_j2, pos_i2, P - 1, None, ALU.bitwise_and))
                after(nc.vector.tensor_scalar(lane_f, pos_j2, 1.0, None, ALU.add))
                after(nc.vector.tensor_scalar(pos_i2, pos_i2, 7, None, ALU.logical_shift_right))
                after(nc.vector.tensor_copy(tile_f, pos_i2))
                after(nc.vector.tensor_scalar(hi2[:, T_IN:T_ALL], hi2[:, T_IN:T_ALL], 64.0, 4096.0, ALU.is_ge, ALU.mult))
                after(nc.vector.tensor_tensor(tile_f[:, T_IN:T_ALL], tile_f[:, T_IN:T_ALL], hi2[:, T_IN:T_ALL], ALU.add))
                after(nc.vector.tensor_scalar(pos_i2, src_i, 2, None, ALU.logical_shift_right))
                after(nc.vector.tensor_copy(v_a, pos_i2))
                after(nc.vector.tensor_scalar(pos_i2, src_i, 3, None, ALU.bitwise_and))
                after(nc.vector.tensor_scalar(pos_j2, dst_i, P - 1, None, ALU.bitwise_and))
                after(nc.vector.tensor_scalar(pos2, pos_i2, 256.0, 1.0, ALU.mult, ALU.add))
                after(nc.vector.tensor_tensor(v_b, pos2, pos_j2, ALU.add))

                def hots(t, s, used):
                    if used is not None:
                        dve.wait_ge(s_list, used)
                    col = bass.ds(t, 1)
                    nc.vector.tensor_scalar(hot_tile[:, s, :], iota_t[:], tile_f[:, col], None, ALU.is_equal)
                    for k, v in enumerate((v_a, v_b)):
                        last = nc.vector.tensor_scalar(hot_lane[:, s, k, :], iota1h[:], lane_f[:, col], v[:, col], ALU.is_equal, ALU.mult)
                    last.then_inc(s_hot, 1)

                for t in range(UL):
                    hots(t, t % 2, t - 1 if t >= 2 else None)
                with dve.Fori(1, T_IN // UL) as it:
                    for k in range(UL):
                        hots(it * UL + k, k % 2, it * UL + (k - 1))
                hots(T_IN, T_IN % 2, T_IN - 1)
                dve.wait_ge(s_list, T_ALL)
                both = psum[:, 4:8, 0:HALF]
                after(nc.vector.tensor_copy(l_a.rearrange("p (a n) -> p a n", a=2), both[:, 0:2, :]))
                after(nc.vector.tensor_copy(l_b.rearrange("p (a n) -> p a n", a=2), both[:, 2:4, :]))
                after(nc.vector.tensor_scalar(l_c, l_b, 255, None, ALU.bitwise_and))
                after(nc.vector.tensor_copy(l1_loc[:], l_c))
                after(nc.vector.tensor_scalar(l_c, l_b, 8, None, ALU.logical_shift_right))
                after(nc.vector.scalar_tensor_tensor(l1_idx[:], l_a, 4.0, l_c, ALU.mult, ALU.add))

            @block.tensor
            def _(pe):
                pt2(pe)

                def product(t1, s, start, stop):
                    pe.wait_ge(s_hot, t1)
                    for k in range(2):
                        for h in range(2):
                            last = nc.tensor.matmul(bank(4 + 2 * k + h)[:, 0:HALF], hot_lane[:, s, k, :],
                                                    hot_tile[:, s, h * HALF:(h + 1) * HALF], start=start, stop=stop)
                    last.then_inc(s_list, 1)

                for t in range(UL):
                    product(t + 1, t % 2, t == 0, False)
                with pe.Fori(1, T_IN // UL) as it:
                    for k in range(UL):
                        product(it * UL + (k + 1), k % 2, False, False)
                product(T_ALL, T_IN % 2, False, True)

        fresh()
        YG, YS = 4, 4
        Y_GROUPS = SLOTS // YG
        rec = tmp([YS, YG, REC], F32)
        bg = tmp([YS, YG, Z], F32)
        zb = tmp([YS, YG, Z], F32)
        hot = tmp([YS, YG, P], BF16)
        hotT = tmp([YS, YG, P], BF16)
        eT = tmp([YS, YG, P], F32)
        acc = tmp([2, 2 * Z], F32)
        assert cursor[0] <= APARTS_AT, (cursor[0], APARTS_AT)
        s_rl = [sem(f"rec_loaded{i}") for i in range(YS)]
        s_bg = [sem(f"b_gathered{i}") for i in range(YS)]
        s_zs = [sem(f"z_stored{i}") for i in range(YS)]
        s_oh, s_oht, s_ohe, s_et, s_ee = sem("hot"), sem("hot_transposed"), sem("hotT_copied"), sem("e_transposed"), sem("eT_copied")
        s_zp, s_za, s_sq, s_acc, s_accz, s_sl = sem("z_product"), sem("z_added"), sem("z_squared"), sem("squares_added"), sem("z_accumulated"), sem("srcloc_copied")
        s_fin, s_fc, s_gb = sem("sums_done"), sem("stat_chain"), sem("gamma_loaded")
        acc_z = bank(7)
        sums = bank(0)

        with nc.Block() as block:
            @block.sync
            def _(sp):
                with nc.allow_non_contiguous_dma(reason="two short vectors, once"):
                    sp.dma_start(stat[:, 4:6], gamma0.rearrange("(h p) -> p h", p=P)).then_inc(s_gb, 16)
                    sp.dma_start(stat[:, 6:8], beta0.rearrange("(h p) -> p h", p=P)).then_inc(s_gb, 16)

                def load(g, s, use):
                    wait(sp, s_bg[s], (use - 1) * (16 * YG))
                    settle(sp, s_sp_turn)
                    for done in (s_sl, s_oh, s_et):
                        wait(sp, done, g - 3)
                        settle(sp, s_sp_turn)
                    sp.dma_start(rec[:, s, :, :], rec_d[:, bass.ds(g * YG, YG), :]).then_inc(s_rl[s], 16)

                groups(sp, load, None, Y_GROUPS, YS)

            @block.gpsimd
            def _(pool):
                def gather(g, s, use):
                    wait(pool, s_rl[s], use * 16)
                    wait(pool, s_za, 2 * g - 6)
                    settle(pool, s_turn)
                    for k in range(YG):
                        nc.gpsimd.indirect_dma_start(bg[:, s, k, :], None, b_tab,
                                                     bass.IndirectOffsetOnAxis(rec[:, s, k, H:H + 1].bitcast(I32), 0)).then_inc(s_bg[s], 16)

                groups(pool, gather, None, Y_GROUPS, YS)
                for s in range(YS):
                    pool.wait_ge(s_bg[s], (Y_GROUPS // YS) * 16 * YG)

            @block.vector
            def _(dve):
                def hots(g, s, use):
                    wait(dve, s_rl[s], use * 16)
                    wait(dve, s_oht, g - 3)
                    for k in range(YG):
                        last = nc.vector.tensor_scalar(hot[:, s, k, :], iota1b[:], rec[:, s, k, H + 1:H + 2], None, ALU.is_equal)
                    last.then_inc(s_oh, 1)

                def add(g, s, use):
                    wait(dve, s_bg[s], use * (16 * YG))
                    wait(dve, s_zs[s], (use - 1) * 16)
                    for q in range(2):
                        wait(dve, s_zp, 2 * g + (q + 1))
                        nc.vector.tensor_tensor(zb[:, s, 2 * q:2 * q + 2, :].rearrange("p a z -> p (a z)"), bank(3 + q % 2),
                                                bg[:, s, 2 * q:2 * q + 2, :].rearrange("p a z -> p (a z)"), ALU.add).then_inc(s_za, 1)
                        if q >= 1 or not (isinstance(g, int) and g == 0):
                            accumulate(2 * g + (q - 1), 1 - q)
                        wait(dve, s_za, 2 * g + (q + 1))
                        wait(dve, s_accz, 2 * g + (q + 1))
                        nc.vector.tensor_tensor(acc_z, zb[:, s, 2 * q:2 * q + 2, :].rearrange("p a z -> p (a z)"), acc_z, ALU.add).then_inc(s_accz, 1)

                def accumulate(n, b):
                    wait(dve, s_sq, n + 1)
                    wait(dve, s_acc, n + 1)
                    nc.vector.tensor_tensor(acc[:, 0, :], bank(5 + b), acc[:, 0, :], ALU.add).then_inc(s_acc, 1)

                nc.vector.memset(acc[:, 0, :], 0.0).then_inc(s_acc, 1)
                nc.vector.memset(acc_z, 0.0).then_inc(s_accz, 1)
                groups(dve, hots, add, Y_GROUPS, YS, lag=2)
                accumulate(2 * Y_GROUPS - 1, 1)
                dve.wait_ge(s_accz, 2 * Y_GROUPS + 1)
                nc.vector.tensor_copy(acc[:, 1, :], acc_z).then_inc(s_accz, 1)
                n = [0]

                def after(ins):
                    n[0] += 1
                    ins.then_inc(s_fc, 1)
                    dve.wait_ge(s_fc, n[0])

                dve.wait_ge(s_gb, 32)
                dve.wait_ge(s_fin, 1)
                mean, ex2, var = stat[:, 8:10], stat[:, 10:12], stat[:, 12:14]
                after(nc.vector.tensor_scalar(mean, sums[:, 0:2], 1.0 / N_EDGES, None, ALU.mult))
                after(nc.vector.tensor_scalar(ex2, sums[:, 2:4], 1.0 / N_EDGES, None, ALU.mult))
                after(nc.vector.tensor_tensor(var, mean, mean, ALU.mult))
                after(nc.vector.tensor_tensor(var, ex2, var, ALU.subtract))
                after(nc.vector.tensor_scalar(var, var, 0.0, BN_EPS, ALU.max, ALU.add))
                dve.wait_ge(s_fin, 2)
                after(nc.vector.reciprocal(ex2, var))
                after(nc.vector.tensor_tensor(bn_s, ex2, stat[:, 4:6], ALU.mult))
                after(nc.vector.tensor_tensor(mean, mean, bn_s, ALU.mult))
                after(nc.vector.tensor_tensor(bn_t, stat[:, 6:8], mean, ALU.subtract))
                after(nc.vector.tensor_scalar(stat[:, 4:5], bn_s[:, 0:1], -1.0, None, ALU.mult))
                after(nc.vector.tensor_scalar(stat[:, 5:6], bn_t[:, 0:1], -1.0, None, ALU.mult))

            @block.scalar
            def _(act):
                def copies(g, s, use):
                    wait(act, s_rl[s], use * 16)
                    nc.scalar.activation(srcloc[:, bass.ds(g * YG, YG)], rec[:, s, :, H + 1:H + 2].rearrange("p g a -> p (g a)"), ACT.Copy).then_inc(s_sl, 1)
                    wait(act, s_oht, g + 1)
                    wait(act, s_zp, 2 * g - 6)
                    nc.scalar.activation(hotT[:, s, :, :].rearrange("p g n -> p (g n)"), bank(0).bitcast(BF16)[:, 0:YG * P], ACT.Copy).then_inc(s_ohe, 1)
                    wait(act, s_et, g + 1)
                    nc.scalar.activation(eT[:, s, :, :].rearrange("p g n -> p (g n)"), bank(1 + s % 2), ACT.Copy).then_inc(s_ee, 1)

                def square(g, s, use):
                    for q in range(2):
                        wait(act, s_za, 2 * g + (q + 1))
                        wait(act, s_acc, 2 * g + q)
                        nc.scalar.activation(bank(5 + q % 2), zb[:, s, 2 * q:2 * q + 2, :].rearrange("p a z -> p (a z)"), ACT.Square).then_inc(s_sq, 1)
                    act.dma_start(z_d[:, bass.ds(g * YG, YG), :], zb[:, s, :, :]).then_inc(s_zs[s], 16)

                groups(act, copies, square, Y_GROUPS, YS, lag=2)
                for s in range(YS):
                    act.wait_ge(s_zs[s], (Y_GROUPS // YS) * 16)
                act.wait_ge(s_fc, 5)
                nc.scalar.activation(stat[:, 12:14], stat[:, 12:14], ACT.Sqrt).then_inc(s_fin, 1)

            @block.tensor
            def _(pe):
                def transposes(g, s, use):
                    wait(pe, s_oh, g + 1)
                    wait(pe, s_ohe, g)
                    for k in range(YG):
                        last = nc.tensor.transpose(bank(0).bitcast(BF16)[:, k * P:(k + 1) * P], hot[:, s, k, :], identb[:])
                    last.then_inc(s_oht, 1)
                    wait(pe, s_rl[s], use * 16)
                    wait(pe, s_ee, g - 1)
                    for k in range(YG):
                        last = nc.tensor.transpose(bank(1 + s % 2)[:, k * P:(k + 1) * P], rec[:, s, k, 0:H], ident[:])
                    last.then_inc(s_et, 1)

                def product(g, s, use):
                    _, blocks = nc.values_load_multi_w_load_instructions(
                        blk_row[0:1, 0, bass.ds(g * YG, YG)], engines=[PE_ENGINE], min_val=0, max_val=BLOCKS - 1,
                        skip_runtime_bounds_check_because="the ids are clamped when made")
                    wait(pe, s_ohe, g + 1)
                    wait(pe, s_ee, g + 1)
                    for q in range(2):
                        wait(pe, s_za, 2 * g + (q - 1))
                        for a in range(2):
                            k = 2 * q + a
                            zp = bank(3 + q % 2)[:, a * Z:(a + 1) * Z]
                            nc.tensor.matmul(zp, eT[:, s, k, :], weT[:], start=True, stop=False)
                            for part in range(3):
                                rhs = aparts[:, bass.ds(blocks[k], 1), part, :].rearrange("p a z -> p (a z)")
                                last = nc.tensor.matmul(zp, hotT[:, s, k, :], rhs, start=False, stop=(part == 2))
                        last.then_inc(s_zp, 1)

                groups(pe, transposes, product, Y_GROUPS, YS)
                pe.wait_ge(s_acc, 2 * Y_GROUPS + 1)
                pe.wait_ge(s_accz, 2 * Y_GROUPS + 2)
                pe.wait_ge(s_ohe, Y_GROUPS)
                for h in range(2):
                    for col, which in ((h, 1), (2 + h, 0)):
                        for a in range(2):
                            last = nc.tensor.matmul(sums[:, col:col + 1], acc[:, which, a * Z + h * H:a * Z + (h + 1) * H], ones[:, 0:1],
                                                    start=(a == 0), stop=(a == 1))
                last.then_inc(s_fin, 1)

        AT_EXP, AT_HOLD, AT_LOG, AT_MAX, AT_MULT, AT_BACK, AT_COPY, AT_SUM, AT_ADD = range(1, 10)
        fresh()
        zl = tmp([2, G, Z], F32)
        hotf = tmp([4, 4, P], F32)
        vaf, sig = tmp([4, 4 * P], F32), tmp([4, 4 * P], F32)
        spl, mT, msg = (tmp([2, 4 * P], F32) for _ in range(3))
        ex = tmp([4, 8 * P], F32)
        agg = tmp([2, BLOCKS, H], F32)
        N_HALVES = 2 * N_GROUPS
        EXP_MAX = 2.0 ** 62
        LOG, BACK, SUMS = 4, 6, 7
        s_zl = [sem(f"z_loaded{i}") for i in range(2)]
        (s_hf, s_zt, s_ex, s_va, s_cl, s_lg, s_sig, s_spl, s_msgT, s_mt, s_mc, s_sc, s_fl) = (
            sem(n) for n in ("hot32", "z_transposed", "exps", "v_scaled", "exps_held", "logs", "sigmoid",
                             "softplus", "messageT", "message_transposed", "message_copied", "segment_product", "segment_added"))

        def halves(eng, step, lag):
            for m in range(12):
                step(m, m % 4, m // 4)
            with eng.Fori(3, N_HALVES // 4) as it:
                for j in range(4):
                    step(4 * it + j, j, it)
            for m in range(N_HALVES, N_HALVES + lag):
                step(m, m % 4, m // 4)

        def there(n):
            return not isinstance(n, int) or 0 <= n < N_HALVES

        with nc.Block() as block:
            @block.sync
            def _(sp):
                def load(g, s, use):
                    wait(sp, s_zt, 2 * g - 2)
                    settle(sp, s_sp_turn)
                    sp.dma_start(zl[:, s, :, :], z_d[:, bass.ds(g * G, G), :]).then_inc(s_zl[s], 16)

                groups(sp, load, None, N_GROUPS, 2)

            @block.tensor
            def _(pe):
                def step(m, j, it):
                    if there(m):
                        h, s = j % 2, j // 2
                        wait(pe, s_zl[s], it * 16 + 16)
                        wait(pe, s_ex, 2 * m - 2)
                        wait(pe, s_va, m - 1)
                        for part in range(2):
                            for k in range(4):
                                last = nc.tensor.transpose(bank(2 * h + 1 - part)[:, k * P:(k + 1) * P],
                                                           zl[:, s, 4 * h + k, part * H:(part + 1) * H], ident[:])
                        last.then_inc(s_zt, 1)
                    n, h = m - AT_BACK, (j - AT_BACK) % 2
                    if there(n):
                        wait(pe, s_msgT, n + 1)
                        wait(pe, s_mc, n)
                        for k in range(4):
                            last = nc.tensor.transpose(bank(BACK)[:, k * P:(k + 1) * P], mT[:, h, k * P:(k + 1) * P], ident[:])
                        last.then_inc(s_mt, 1)
                    n, h, r = m - AT_SUM, (j - AT_SUM) % 2, (j - AT_SUM) % 4
                    if there(n):
                        wait(pe, s_mc, n + 1)
                        wait(pe, s_hf, n + 1)
                        wait(pe, s_fl, 4 * n + 2)
                        for k in range(4):
                            last = nc.tensor.matmul(bank(SUMS)[:, k * P:(k + 1) * P], hotf[:, r, k, :],
                                                    msg[:, h, k * P:(k + 1) * P], start=True, stop=True)
                        last.then_inc(s_sc, 1)

                halves(pe, step, AT_SUM)

            @block.scalar
            def _(act):
                def step(m, j, it):
                    n, h, r = m - AT_EXP, (j - AT_EXP) % 2, (j - AT_EXP) % 4
                    if there(n):
                        wait(act, s_zt, n + 1)
                        wait(act, s_lg, n - 3)
                        nc.scalar.activation(ex[:, r, 0:4 * P], bank(2 * h), ACT.Exp, bias=bn_t[:, 1:2], scale=bn_s[:, 1:2]).then_inc(s_ex, 1)
                        nc.scalar.activation(ex[:, r, 4 * P:8 * P], bank(2 * h + 1), ACT.Exp, bias=stat[:, 5:6], scale=stat[:, 4:5]).then_inc(s_ex, 1)
                        wait(act, s_spl, n - 3)
                        nc.scalar.activation(vaf[:, r, :], bank(2 * h), ACT.Identity, bias=bn_t[:, 1:2], scale=bn_s[:, 1:2]).then_inc(s_va, 1)
                    n, r = m - AT_LOG, (j - AT_LOG) % 4
                    if there(n):
                        wait(act, s_cl, n + 1)
                        wait(act, s_spl, n)
                        wait(act, s_sig, n)
                        nc.scalar.activation(psum[:, LOG:LOG + 2, :].rearrange("p a n -> p (a n)"), ex[:, r, :], ACT.Ln, bias=1.0).then_inc(s_lg, 1)
                        wait(act, s_lg, n + 1)
                        wait(act, s_msgT, n - 3)
                        nc.scalar.activation(sig[:, r, :], bank(LOG + 1), ACT.Exp, scale=-1.0).then_inc(s_sig, 1)

                act.preload_act_table_set("natural_log_exp_and_others")
                halves(act, step, AT_LOG)

            @block.gpsimd
            def _(pool):
                def step(m, j, it):
                    n, h, r = m - AT_MULT, (j - AT_MULT) % 2, (j - AT_MULT) % 4
                    if there(n):
                        wait(pool, s_spl, n + 1)
                        wait(pool, s_sig, n + 1)
                        wait(pool, s_mt, n - 1)
                        nc.gpsimd.tensor_tensor(mT[:, h, :], spl[:, h, :], sig[:, r, :], ALU.mult).then_inc(s_msgT, 1)

                halves(pool, step, AT_MULT)

            @block.vector
            def _(dve):
                def step(m, j, it):
                    n, h, r = m - AT_MAX, (j - AT_MAX) % 2, (j - AT_MAX) % 4
                    if there(n):
                        wait(dve, s_lg, n + 1)
                        wait(dve, s_va, n + 1)
                        wait(dve, s_msgT, n - 1)
                        nc.vector.tensor_tensor(spl[:, h, :], bank(LOG), vaf[:, r, :], ALU.max).then_inc(s_spl, 1)
                    n, h = m - AT_COPY, (j - AT_COPY) % 2
                    if there(n):
                        wait(dve, s_mt, n + 1)
                        wait(dve, s_sc, n - 1)
                        nc.vector.tensor_copy(msg[:, h, :], bank(BACK)).then_inc(s_mc, 1)
                    n = m - AT_ADD
                    if there(n):
                        _, blocks = nc.values_load_multi_w_load_instructions(
                            blk_row[0:1, 0, bass.ds(n * 4, 4)], engines=[DVE_ENGINE], min_val=0, max_val=BLOCKS - 1,
                            skip_runtime_bounds_check_because="the ids are clamped when made")
                        wait(dve, s_sc, n + 1)
                        for k in range(4):
                            wait(dve, s_fl, 4 * n + (k - 1) + 2)
                            dest = agg[:, k % 2, bass.ds(blocks[k], 1), :].rearrange("p a f -> p (a f)")
                            nc.vector.tensor_tensor(dest, bank(SUMS)[:, k * P:(k + 1) * P], dest, ALU.add).then_inc(s_fl, 1)
                    n, r = m - AT_HOLD, (j - AT_HOLD) % 4
                    if there(n):
                        wait(dve, s_ex, 2 * n + 2)
                        nc.vector.tensor_scalar(ex[:, r, :], ex[:, r, :], EXP_MAX, None, ALU.min).then_inc(s_cl, 1)
                    n, r = m - AT_COPY, (j - AT_COPY) % 4
                    if there(n):
                        wait(dve, s_sc, n - 3)
                        for k in range(4):
                            col = srcloc[:, n * 4 + k:n * 4 + k + 1] if isinstance(n, int) else srcloc[:, bass.ds(n * 4 + k, 1)]
                            last = nc.vector.tensor_scalar(hotf[:, r, k, :], iota1[:], col, None, ALU.is_equal)
                        last.then_inc(s_hf, 1)

                nc.vector.memset(agg[:, 0, :, :], 0.0).then_inc(s_fl, 1)
                nc.vector.memset(agg[:, 1, :, :], 0.0).then_inc(s_fl, 1)
                halves(dve, step, AT_ADD)

        fl = lambda v: v.rearrange("p b f -> p (b f)")
        x1 = tmp([BLOCKS, H + 1], F32)
        red = tmp([8, BLOCKS], F32)
        s_n, s_nq, s_xs = sem("norm0_chain"), sem("norm0_root"), sem("x1_stored")

        def bc(v):
            return v.unsqueeze(2).broadcast_to([P, BLOCKS, H])

        def layernorm(after, root, y, scr, eps):
            mean, var, rs = red[:, 0, :], red[:, 1, :], red[:, 2, :]
            after(nc.vector.tensor_reduce(mean, y, op=ALU.add, axis=AX_X))
            after(nc.vector.tensor_scalar(mean, mean, 1.0 / H, None, ALU.mult))
            after(nc.vector.tensor_tensor(y, y, bc(mean), ALU.subtract))
            after(nc.vector.tensor_tensor(scr, y, y, ALU.mult))
            after(nc.vector.tensor_reduce(var, scr, op=ALU.add, axis=AX_X))
            after(nc.vector.tensor_scalar(var, var, 1.0 / H, eps, ALU.mult, ALU.add))
            root()
            after(nc.vector.reciprocal(rs, var))
            after(nc.vector.tensor_tensor(y, y, bc(rs), ALU.mult))

        with nc.Block() as block:
            @block.vector
            def _(dve):
                n = [0]

                def after(ins):
                    n[0] += 1
                    ins.then_inc(s_n, 1)
                    dve.wait_ge(s_n, n[0])

                def root():
                    dve.sem_inc(s_nq, 1)
                    dve.wait_ge(s_nq, 2)

                y = agg[:, 0, :, :]
                after(nc.vector.tensor_tensor(y, y, agg[:, 1, :, :], ALU.add))
                after(nc.vector.scalar_tensor_tensor(fl(y), fl(x_sb[:]), 2.0, fl(y), ALU.mult, ALU.add))
                layernorm(after, root, y, agg[:, 1, :, :], LN_EPS)
                after(nc.vector.memset(x1[:, :, H:H + 1], 1.0))
                after(nc.vector.tensor_copy(x1[:, :, 0:H], y))
                dve.sem_inc(s_nq, 1)

            @block.scalar
            def _(act):
                act.wait_ge(s_nq, 1)
                nc.scalar.activation(red[:, 1, :], red[:, 1, :], ACT.Sqrt).then_inc(s_nq, 1)

            @block.sync
            def _(sp):
                sp.wait_ge(s_nq, 3)
                sp.dma_start(x1_tab.rearrange("(b p) f -> p b f", p=P), x1).then_inc(s_xs, 16)
                sp.wait_ge(s_xs, 16)

        x1_at = cursor[0] - 8 * BLOCKS - BLOCKS * (H + 1)
        fresh()
        xg = tmp([2, G, H + 1], F32)
        hotg = tmp([2, G, P], F32)
        gi = tmp([2, G], I32)
        gl = tmp([2, G], F32)
        agg1 = tmp([2, BLOCKS, H + 1], F32)
        assert cursor[0] <= x1_at, (cursor[0], x1_at)
        s_xg = [sem(f"x1_gathered{i}") for i in range(2)]
        s_gi, s_hg, s_sg, s_fg = sem("list_columns"), sem("hot_by_dst"), sem("average_product"), sem("average_added")

        with nc.Block() as block:
            @block.scalar
            def _(act):
                def columns(g, s, use):
                    wait(act, s_xg[s], (use - 1) * (16 * G))
                    wait(act, s_hg, g - 1)
                    nc.scalar.activation(gi[:, s, :], l1_idx[:, bass.ds(g * G, G)], ACT.Copy).then_inc(s_gi, 1)
                    nc.scalar.activation(gl[:, s, :], l1_loc[:, bass.ds(g * G, G)], ACT.Copy).then_inc(s_gi, 1)

                groups(act, columns, None, N_GROUPS, 2)

            @block.gpsimd
            def _(pool):
                def gather(g, s, use):
                    wait(pool, s_gi, 2 * g + 2)
                    wait(pool, s_sg, 4 * g - 4)
                    settle(pool, s_turn)
                    for k in range(G):
                        nc.gpsimd.indirect_dma_start(xg[:, s, k, :], None, x1_tab, bass.IndirectOffsetOnAxis(gi[:, s, k:k + 1], 0)).then_inc(s_xg[s], 16)

                groups(pool, gather, None, N_GROUPS, 2)

            @block.tensor
            def _(pe):
                def product(g, s, use):
                    wait(pe, s_hg, g + 1)
                    wait(pe, s_xg[s], use * (16 * G))
                    for q in range(4):
                        wait(pe, s_fg, 8 * g - 16 + 2 * q + 4)
                        for a in range(2):
                            last = nc.tensor.matmul(bank(4 * s + q)[:, a * 256:a * 256 + H + 1], hotg[:, s, 2 * q + a, :], xg[:, s, 2 * q + a, :],
                                                    start=True, stop=True)
                        last.then_inc(s_sg, 1)

                groups(pe, product, None, N_GROUPS, 2)

            @block.vector
            def _(dve):
                def hots(g, s, use):
                    wait(dve, s_gi, 2 * g + 2)
                    wait(dve, s_sg, 4 * g - 4)
                    for k in range(G):
                        last = nc.vector.tensor_scalar(hotg[:, s, k, :], iota1[:], gl[:, s, k:k + 1], None, ALU.is_equal)
                    last.then_inc(s_hg, 1)

                def add(g, s, use):
                    _, blocks = nc.values_load_multi_w_load_instructions(
                        blk_row[0:1, 1, bass.ds(g * G, G)], engines=[DVE_ENGINE], min_val=0, max_val=BLOCKS - 1,
                        skip_runtime_bounds_check_because="the ids are clamped when made")
                    for q in range(4):
                        wait(dve, s_sg, 4 * g + (q + 1))
                        for a in range(2):
                            k = 2 * q + a
                            wait(dve, s_fg, 8 * g + (k + 1))
                            dest = agg1[:, a, bass.ds(blocks[k], 1), :].rearrange("p a f -> p (a f)")
                            nc.vector.tensor_tensor(dest, bank(4 * s + q)[:, a * 256:a * 256 + H + 1], dest, ALU.add).then_inc(s_fg, 1)

                nc.vector.memset(agg1[:, 0, :, :], 0.0).then_inc(s_fg, 1)
                nc.vector.memset(agg1[:, 1, :, :], 0.0).then_inc(s_fg, 1)
                groups(dve, hots, add, N_GROUPS, 2)

        x1T = x_sb
        enh = tmp([BLOCKS, H], F32)
        w1s = tmp([64], F32)
        w2s = tmp([H], F32)
        b1s = tmp([1], F32)
        bc3 = tmp([3, H], F32)
        hT = tmp([2, 512], F32)
        assert cursor[0] <= x1_at
        s_wl, s_t1, s_t1c, s_m1, s_m1c, s_m2, s_m2c = (sem(n) for n in (
            "w12_loaded", "x1_transposed", "x1T_copied", "mlp1", "mlp1_relu", "mlp2", "mlp2_copied"))
        s_f, s_fq, s_fc2, s_out = sem("finish_chain"), sem("finish_asked"), sem("finish_root"), sem("out_stored")
        CH = [(b, min(4, BLOCKS - b)) for b in range(0, BLOCKS, 4)]

        with nc.Block() as block:
            @block.sync
            def _(sp):
                sp.dma_start(w1s, W1).then_inc(s_wl, 16)
                sp.dma_start(w2s[0:64, :], W2).then_inc(s_wl, 16)
                with nc.allow_non_contiguous_dma(reason="a column, once"):
                    sp.dma_start(b1s[0:64, :], b1.rearrange("(p a) -> p a", a=1)).then_inc(s_wl, 16)
                for i, v in enumerate((b2, gamma1, beta1)):
                    sp.dma_start(bc3[:, i, :], v.rearrange("(a n) -> a n", a=1).broadcast_to([P, H])).then_inc(s_wl, 16)
                sp.wait_ge(s_fq, 5)
                sp.dma_start(out[0:(BLOCKS - 1) * P, :].rearrange("(b p) f -> p b f", p=P), enh[:, 0:BLOCKS - 1, :]).then_inc(s_out, 16)
                sp.dma_start(out[(BLOCKS - 1) * P:N_NODES, :], enh[0:LAST, BLOCKS - 1, :]).then_inc(s_out, 16)
                sp.wait_ge(s_out, 32)

            @block.tensor
            def _(pe):
                pe.wait_ge(s_wl, 16 * 6)
                for c, (b0, nb) in enumerate(CH):
                    if c >= 2:
                        pe.wait_ge(s_t1c, c - 1)
                    for k in range(nb):
                        last = nc.tensor.transpose(bank(c % 2)[:, k * P:(k + 1) * P], x1[:, b0 + k, 0:H], ident[:])
                    last.then_inc(s_t1, 1)
                for c, (b0, nb) in enumerate(CH):
                    pe.wait_ge(s_t1c, c + 1)
                    if c >= 2:
                        pe.wait_ge(s_m1c, c - 1)
                    nc.tensor.matmul(bank(2 + c % 2)[0:64, 0:nb * P], w1s, x1T[:, b0:b0 + nb, :].rearrange("p b n -> p (b n)"),
                                     start=True, stop=True).then_inc(s_m1, 1)
                    pe.wait_ge(s_m1c, c + 1)
                    if c >= 2:
                        pe.wait_ge(s_m2c, c - 1)
                    for k in range(nb):
                        last = nc.tensor.matmul(bank(4 + c % 2)[:, k * P:(k + 1) * P], hT[0:64, c % 2, k * P:(k + 1) * P], w2s[0:64, :],
                                                start=True, stop=True)
                    last.then_inc(s_m2, 1)

            @block.scalar
            def _(act):
                act.wait_ge(s_wl, 16 * 6)
                for c, (b0, nb) in enumerate(CH):
                    act.wait_ge(s_t1, c + 1)
                    nc.scalar.activation(x1T[:, b0:b0 + nb, :].rearrange("p b n -> p (b n)"), bank(c % 2)[:, 0:nb * P], ACT.Copy).then_inc(s_t1c, 1)
                for c, (b0, nb) in enumerate(CH):
                    act.wait_ge(s_m1, c + 1)
                    if c >= 2:
                        act.wait_ge(s_m2, c - 1)
                    nc.scalar.activation(hT[0:64, c % 2, 0:nb * P], bank(2 + c % 2)[0:64, 0:nb * P], ACT.Relu, bias=b1s[0:64, :]).then_inc(s_m1c, 1)
                    act.wait_ge(s_m2, c + 1)
                    nc.scalar.activation(enh[:, b0:b0 + nb, :].rearrange("p b n -> p (b n)"), bank(4 + c % 2)[:, 0:nb * P], ACT.Copy).then_inc(s_m2c, 1)
                dist = red[:, 3, :]
                act.wait_ge(s_fq, 1)
                nc.scalar.activation(dist, dist, ACT.Sqrt).then_inc(s_fc2, 1)
                act.wait_ge(s_fc2, 1)
                nc.scalar.activation(dist, dist, ACT.Tanh).then_inc(s_fq, 1)
                act.wait_ge(s_fq, 3)
                nc.scalar.activation(red[:, 1, :], red[:, 1, :], ACT.Sqrt).then_inc(s_fc2, 1)
                act.wait_ge(s_fq, 4)
                nc.scalar.activation(red[:, 1, :], red[:, 1, :], ACT.Sqrt).then_inc(s_fc2, 1)

            @block.vector
            def _(dve):
                n = [0]

                def after(ins):
                    n[0] += 1
                    ins.then_inc(s_f, 1)
                    dve.wait_ge(s_f, n[0])

                roots = [1]

                def root():
                    dve.sem_inc(s_fq, 1)
                    roots[0] += 1
                    dve.wait_ge(s_fc2, roots[0])

                sm, sc = agg1[:, 0, :, :], agg1[:, 1, :, :]
                cntv = red[:, 4, :]
                after(nc.vector.tensor_tensor(sm, sm, sc, ALU.add))
                after(nc.vector.tensor_scalar(cntv, sm[:, :, H:H + 1].rearrange("p b a -> p (b a)"), 1.0, None, ALU.max))
                after(nc.vector.reciprocal(cntv, cntv))
                after(nc.vector.tensor_tensor(sm[:, :, 0:H], sm[:, :, 0:H], bc(cntv), ALU.mult))
                after(nc.vector.tensor_tensor(sm[:, :, 0:H], x1[:, :, 0:H], sm[:, :, 0:H], ALU.subtract))
                after(nc.vector.tensor_tensor(sm[:, :, 0:H], sm[:, :, 0:H], sm[:, :, 0:H], ALU.mult))
                after(nc.vector.tensor_reduce(red[:, 3, :], sm[:, :, 0:H], op=ALU.add, axis=AX_X))
                dve.sem_inc(s_fq, 1)
                bcv = lambda i: bc3[:, i, :].unsqueeze(1).broadcast_to([P, BLOCKS, H])
                dve.wait_ge(s_m2c, len(CH))
                after(nc.vector.tensor_tensor(enh, enh, bcv(0), ALU.add))
                dve.wait_ge(s_fq, 2)
                after(nc.vector.tensor_scalar(red[:, 3, :], red[:, 3, :], ALPHA, None, ALU.mult))
                after(nc.vector.tensor_tensor(enh, enh, bc(red[:, 3, :]), ALU.mult))
                after(nc.vector.tensor_tensor(enh, enh, x1[:, :, 0:H], ALU.add))
                layernorm(after, root, enh, x_sb[:], LN_EPS)
                after(nc.vector.tensor_tensor(enh, enh, bcv(1), ALU.mult))
                after(nc.vector.tensor_tensor(enh, enh, bcv(2), ALU.add))
                after(nc.vector.tensor_tensor(enh, enh, x1[:, :, 0:H], ALU.add))
                layernorm(after, root, enh, x_sb[:], LN_EPS)
                dve.sem_inc(s_fq, 1)



_INS = ["x", "src", "dst", "edge_attr_128", "L0_gnn_W", "L0_gnn_b", "L0_gnn_gamma", "L0_gnn_beta",
        "L1_gnn_W1", "L1_gnn_b1", "L1_gnn_W2", "L1_gnn_b2", "L1_gnn_gamma", "L1_gnn_beta"]


def kernel(**inputs):
    import numpy as _np
    import concourse.bacc as _bacc
    from concourse import mybir as _mybir
    from concourse.bass_utils import run_bass_kernel_spmd as _run

    nc = _bacc.Bacc("TRN2", target_bir_lowering=False, num_devices=1)
    arrays, args = {}, []
    for name in _INS:
        a = _np.ascontiguousarray(inputs[name])
        arrays[f"in_{name}"] = a
        args.append(nc.dram_tensor(f"in_{name}", a.shape, _mybir.dt.from_np(a.dtype), kind="ExternalInput").ap())
    args.append(nc.dram_tensor("out_0", (N_NODES, H), _mybir.dt.float32, kind="ExternalOutput").ap())
    build(nc, *args)
    r = _run(nc, [arrays], core_ids=[0])
    return r.results[0]["out_0"]
```

```python
from contextlib import ExitStack

import concourse.bass as bass
from concourse import mybir

ALU = mybir.AluOpType
ACT = mybir.ActivationFunctionType
AX_X = mybir.AxisListType.X
F32 = mybir.dt.float32
BF16 = mybir.dt.bfloat16
I32 = mybir.dt.int32
I16 = mybir.dt.int16
F16 = mybir.dt.float16
PE_ENGINE = mybir.EngineType.PE
DVE_ENGINE = mybir.EngineType.DVE

P = 128
N_NODES, N_EDGES, H = 6250, 106250, 128
Z = 2 * H
BLOCKS = -(-N_NODES // P)
ROWS = BLOCKS * P
LAST = N_NODES - (BLOCKS - 1) * P
T_IN = N_EDGES // P
TAIL = N_EDGES - P * T_IN
T_ALL = T_IN + 1
G_IN = 10
N_GROUPS_IN = T_IN // G_IN
G = 8
SLOTS = -(-((N_EDGES + BLOCKS * (P - 1)) // P) // (2 * G)) * (2 * G)
N_GROUPS = SLOTS // G
HALF = SLOTS // 2
REC = H + 2
BN_EPS = 1e-5
LN_EPS = 1e-5
ALPHA = 0.2
INVALID = 127 * P


def wait(eng, semaphore, value):
    if not isinstance(value, int) or value > 0:
        eng.wait_ge(semaphore, value)


def settle(eng, turns):
    eng.sem_inc(turns, 1)


def groups(eng, front, back, n, slots, lag=1):
    def turn(g, s, use):
        if not isinstance(g, int) or g < n:
            front(g, s, use)
        if back is not None and not (isinstance(g, int) and g < lag):
            back(g - lag, (s - lag) % slots, use if s >= lag else use - 1)

    for g in range(2 * slots):
        turn(g, g % slots, g // slots + 1)
    with eng.Fori(2, n // slots) as it:
        for s in range(slots):
            turn(slots * it + s, s, it + 1)
    if back is not None:
        for g in range(n, n + lag):
            turn(g, g % slots, g // slots + 1)


def build(nc, x, src, dst, edge, W, bias, gamma0, beta0, W1, b1, W2, b2, gamma1, beta1, out):
    ctx = ExitStack()
    with ctx:
        def sb(name, shape, dt):
            return ctx.enter_context(nc.sbuf_tensor(name, shape, dt))

        def sem(name):
            return ctx.enter_context(nc.semaphore(name))

        rec_rows = nc.dram_tensor("rec_d", ((SLOTS + BLOCKS) * P, REC), F32).ap()
        rec_d = rec_rows[0:SLOTS * P].rearrange("(p t) r -> p t r", p=P)
        b_tab = nc.dram_tensor("b_tab", (ROWS, Z), F32).ap()
        z_d = nc.dram_tensor("z_d", (P, SLOTS, Z), F32).ap()
        x1_tab = nc.dram_tensor("x1_tab", (ROWS, H + 1), F32).ap()
        blk_d = nc.dram_tensor("blk_d", (2, P, 7), I32).ap()

        x_sb = sb("x_sb", [P, BLOCKS, H], F32)
        ident = sb("ident", [P, P], F32)
        identb = sb("identb", [P, P], BF16)
        ones = sb("ones", [P, P], F32)
        tri = sb("tri", [P, P], F32)
        iota1 = sb("iota1", [P, P], F32)
        iota1b = sb("iota1b", [P, P], BF16)
        iota1h = sb("iota1h", [P, P], F16)
        iota_t = sb("iota_t", [P, SLOTS], F16)
        row0 = sb("row0", [P, P], F32)
        blk_row = sb("blk_row", [1, 2, P * 7], I32)
        srcloc = sb("srcloc", [P, SLOTS], F32)
        l1_loc = sb("l1_loc", [P, SLOTS], F32)
        l1_idx = sb("l1_idx", [P, SLOTS], I32)
        weT = sb("weT", [P, Z], F32)
        stat = sb("stat", [P, 16], F32)
        bn_s = stat[:, 0:2]
        bn_t = stat[:, 2:4]
        ARENA = 39000
        arena = sb("arena", [P, ARENA], F32)
        cursor = [0]

        def fresh(at=0):
            cursor[0] = at

        def tmp(shape, dt):
            n = 1
            for s in shape:
                n *= s
            words = n if dt in (F32, I32) else -(-n // 2)
            v = arena[:, cursor[0]:cursor[0] + words]
            cursor[0] += words
            assert cursor[0] <= ARENA, cursor[0]
            if dt != F32:
                v = v.bitcast(dt)
                if dt in (BF16, I16, F16):
                    v = v[:, 0:n]
            if len(shape) == 2:
                v = v.rearrange("p (a b) -> p a b", a=shape[0])
            elif len(shape) == 3:
                v = v.rearrange("p (a b c) -> p a b c", a=shape[0], b=shape[1])
            return v

        psum = ctx.enter_context(nc.psum_tensor("psum", [P, 8, 512], F32))

        def bank(i):
            return psum[:, i, :]

        src_i = tmp([T_ALL], I32)
        dst_i = tmp([T_ALL], I32)
        loc1 = tmp([T_ALL], F32)
        row_i = tmp([T_ALL], I32)
        lane_f = tmp([T_ALL], F32)
        tile_f = tmp([T_ALL], F32)
        v_a = tmp([T_ALL], F32)
        v_b = tmp([T_ALL], F32)
        EARLY = cursor[0]

        APARTS_AT = ARENA - BLOCKS * 3 * Z // 2
        aparts = arena[:, APARTS_AT:ARENA].bitcast(BF16).rearrange("p (b k z) -> p b k z", b=BLOCKS, k=3)

        def place_steps(tag, hi, pos, cnt, offs, h_ring, work, scalar_counts, pads=None):
            s = {n: sem(f"{tag}_{n}") for n in
                 ("hot", "counted", "countedv", "tot", "hot2", "scan", "pick", "chain", "blk", "blkd", "blkr")}
            tiles, tend, tstart, tcmp, blkf, blki, tnum = (
                work[n] for n in ("tiles", "tend", "tstart", "tcmp", "blkf", "blki", "tnum"))

            by_scalar = list(range(0, BLOCKS, 2)) if scalar_counts else []
            by_vector = [b for b in range(BLOCKS) if b not in by_scalar]

            def vector(dve):
                def after(ins):
                    after.n += 1
                    ins.then_inc(s["chain"], 1)
                    dve.wait_ge(s["chain"], after.n)
                after.n = 0

                def count(i):
                    if i >= 2:
                        dve.wait_ge(s["countedv"], i - 1)
                    nc.vector.tensor_scalar(h_ring[:, 2 + i % 2, :], hi, float(by_vector[i]), None, ALU.is_equal, ALU.add,
                                            accum_out=cnt[:, by_vector[i]:by_vector[i] + 1]).then_inc(s["countedv"], 1)

                for i, b in enumerate(by_scalar):
                    if i >= 2:
                        dve.wait_ge(s["counted"], i - 1)
                    nc.vector.tensor_scalar(h_ring[:, i % 2, :], hi, float(b), None, ALU.is_equal).then_inc(s["hot"], 1)
                    if i < len(by_vector):
                        count(i)
                for i in range(len(by_scalar), len(by_vector)):
                    count(i)
                dve.wait_ge(s["tot"], 1)
                total, before = bank(7)[:, 0:BLOCKS], bank(7)[:, 64:64 + BLOCKS]
                after(nc.vector.tensor_scalar(tnum, total, 127.0, None, ALU.add))
                after(nc.vector.tensor_scalar(tnum, tnum, 7, None, ALU.logical_shift_right))
                after(nc.vector.tensor_copy(tiles, tnum))
                after(nc.vector.tensor_tensor_scan(tend, tiles, tiles, 0.0, ALU.add, ALU.bypass))
                after(nc.vector.tensor_tensor(tstart, tend, tiles, ALU.subtract))
                after(nc.vector.tensor_scalar(tstart, tstart, 128.0, -1.0, ALU.mult, ALU.add))
                after(nc.vector.tensor_tensor(offs, before, tstart, ALU.add))
                if pads is not None:
                    pads(after, total, tiles, tend)
                for c in range(7):
                    nc.vector.tensor_scalar(tcmp[:, c, :], tend, work["tile_id"][:, c:c + 1], None, ALU.is_le).then_inc(s["chain"], 1)
                after.n += 7
                dve.wait_ge(s["chain"], after.n)
                after(nc.vector.tensor_reduce(blkf, tcmp, op=ALU.add, axis=AX_X))
                after(nc.vector.tensor_scalar(blkf, blkf, float(BLOCKS - 1), None, ALU.min))
                nc.vector.tensor_copy(blki, blkf).then_inc(s["blk"], 1)
                nc.vector.memset(pos, 0.0).then_inc(s["pick"], 1)
                for b in range(BLOCKS):
                    if b >= 4:
                        dve.wait_ge(s["pick"], b - 2)
                    nc.vector.tensor_scalar(h_ring[:, b % 4, :], hi, float(b), None, ALU.is_equal).then_inc(s["hot2"], 1)
                    scan = psum[:, 2 * (b % 2):2 * (b % 2) + 2, :].rearrange("p a b -> p (a b)")[:, 0:T_ALL]
                    dve.wait_ge(s["hot2"], b + 1)
                    if b >= 2:
                        dve.wait_ge(s["pick"], b)
                    nc.vector.tensor_tensor_scan(scan, h_ring[:, b % 4, :], h_ring[:, b % 4, :], offs[:, b:b + 1],
                                                 ALU.add, ALU.bypass).then_inc(s["scan"], 1)
                    dve.wait_ge(s["scan"], b + 1)
                    dve.wait_ge(s["pick"], b + 1)
                    nc.vector.copy_predicated(pos, h_ring[:, b % 4, :].bitcast(I16), scan).then_inc(s["pick"], 1)
                dve.wait_ge(s["pick"], BLOCKS + 1)

            def scalar(act):
                for i, b in enumerate(by_scalar):
                    act.wait_ge(s["hot"], i + 1)
                    if i >= 2:
                        act.wait_ge(s["counted"], i - 1)
                    nc.scalar.activation(work["junk"][:, i % 2, :], h_ring[:, i % 2, :], ACT.Copy,
                                         accum_out=cnt[:, b:b + 1]).then_inc(s["counted"], 1)

            def tensor(pe):
                if by_scalar:
                    pe.wait_ge(s["counted"], len(by_scalar))
                pe.wait_ge(s["countedv"], len(by_vector))
                nc.tensor.matmul(bank(7)[:, 0:BLOCKS], ones[:], cnt, start=True, stop=True)
                nc.tensor.matmul(bank(7)[:, 64:64 + BLOCKS], tri[:], cnt, start=True, stop=True).then_inc(s["tot"], 1)

            def sync(sp, which):
                sp.wait_ge(s["blk"], 1)
                sp.dma_start(blk_d[which], blki).then_inc(s["blkd"], 16)
                sp.wait_ge(s["blkd"], 16)
                sp.dma_start(blk_row[0:1, which, :], blk_d[which:which + 1].rearrange("a p c -> a (p c)")).then_inc(s["blkr"], 16)
                sp.wait_ge(s["blkr"], 16)

            return vector, scalar, tensor, sync

        def place_work(junk):
            w = dict(tiles=tmp([BLOCKS], F32), tend=tmp([BLOCKS], F32), tstart=tmp([BLOCKS], F32),
                     tcmp=tmp([7, BLOCKS], F32), blkf=tmp([7], F32), blki=tmp([7], I32), tnum=tmp([BLOCKS], I32),
                     tile_id=tmp([7], F32))
            if junk:
                w["junk"] = tmp([2, T_ALL], BF16)
            return w

        fresh(EARLY)
        w_sb = tmp([2, 3 * H], F32)
        wabT = tmp([2 * Z], F32)
        bias_bc = tmp([Z], F32)
        xT = tmp([2, P], F32)
        a_f = tmp([4, Z], F32)
        b_f = tmp([4, Z], F32)
        hi = tmp([T_ALL + 1], F16)[:, 0:T_ALL]
        hi_i = tmp([T_ALL], I32)
        pos = tmp([T_ALL], F32)
        pos_i = tmp([T_ALL], I32)
        h_ring = tmp([4, T_ALL + 1], BF16)[:, :, 0:T_ALL]
        cnt = tmp([BLOCKS], F32)
        offs = tmp([BLOCKS], F32)
        pwork = place_work(True)
        zeros = tmp([REC], F32)
        pad_row = tmp([BLOCKS], F32)
        pad_is = tmp([BLOCKS], F32)
        pad_i = tmp([BLOCKS], I32)
        lane = tmp([1], F32)
        no_row, first_row = tmp([BLOCKS], F32), tmp([BLOCKS], F32)
        assert cursor[0] <= APARTS_AT, (cursor[0], APARTS_AT)

        s_const, s_ci, s_load, s_x, s_w = sem("const"), sem("const_int"), sem("ids_loaded"), sem("x_loaded"), sem("w_loaded")
        s_turn, s_sp_turn = sem("pool_turns"), sem("sync_turns")
        s_tail0 = sem("last_tiles_zeroed")
        s_zero, s_pad, s_padded, s_kc = sem("zeros_ready"), sem("pads_found"), sem("pads_written"), sem("key_chain")
        s_wt, s_we, s_xt, s_xe = sem("w_transposed"), sem("w_copied"), sem("x_transposed"), sem("x_copied")
        s_ab, s_ac, s_bc, s_am = sem("ab_product"), sem("a_copied"), sem("b_copied"), sem("a_middle")
        s_r1, s_sp = sem("a_rest"), sem("a_split")
        s_bst = [sem(f"b_stored{i}") for i in range(4)]
        N_CONST = 14

        def find_pads(after, total, tiles, tend):
            after(nc.vector.scalar_tensor_tensor(pad_is, tiles, float(P), total, ALU.mult, ALU.subtract))
            after(nc.vector.tensor_scalar(pad_is, pad_is, lane, float(P), ALU.add, ALU.is_ge))
            after(nc.vector.tensor_tensor(pad_row, tend, first_row, ALU.add))
            after(nc.vector.tensor_tensor(pad_row, pad_row, pad_is, ALU.mult))
            nc.vector.tensor_tensor(pad_i, pad_row, no_row, ALU.add).then_inc(s_pad, 1)

        pv, pa, pt, ps_ = place_steps("bysrc", hi, pos, cnt, offs, h_ring, pwork, True, find_pads)

        with nc.Block() as block:
            @block.sync
            def _(sp):
                sp.wait_ge(s_ci, 3)
                for ids, col in ((src, src_i), (dst, dst_i)):
                    sp.dma_start(col[:, 0:T_IN], ids[0:P * T_IN].rearrange("(p t) -> p t", p=P)).then_inc(s_load, 16)
                    sp.dma_start(col[0:TAIL, T_IN:T_ALL], ids[P * T_IN:N_EDGES].rearrange("(p t) -> p t", t=1)).then_inc(s_load, 16)
                sp.dma_start(w_sb, W.rearrange("(h p) k -> p h k", p=P)).then_inc(s_w, 16)
                sp.dma_start(bias_bc, bias.rearrange("(a n) -> a n", a=1).broadcast_to([P, Z])).then_inc(s_w, 16)
                sp.dma_start(x_sb[:, 0:BLOCKS - 1, :], x[0:(BLOCKS - 1) * P, :].rearrange("(b p) f -> p b f", p=P)).then_inc(s_x, 16)
                sp.dma_start(x_sb[0:LAST, BLOCKS - 1, :], x[(BLOCKS - 1) * P:N_NODES, :]).then_inc(s_x, 16)
                sp.wait_ge(s_zero, 2)
                sp.dma_start(rec_d[:, T_ALL:SLOTS, :], zeros.unsqueeze(1).broadcast_to([P, SLOTS - T_ALL, REC])).then_inc(s_tail0, 16)
                ps_(sp, 0)
                sp.wait_ge(s_tail0, 16)

            @block.gpsimd
            def _(pool):
                nc.gpsimd.memset(src_i[:, T_IN:T_ALL], INVALID).then_inc(s_ci, 1)
                nc.gpsimd.memset(dst_i[:, T_IN:T_ALL], INVALID).then_inc(s_ci, 1)
                nc.gpsimd.memset(x_sb[:, BLOCKS - 1, :], 0.0).then_inc(s_ci, 1)
                nc.gpsimd.memset(zeros, 0.0).then_inc(s_zero, 1)
                nc.gpsimd.memset(ident[:], 0.0).then_inc(s_const, 1)
                nc.gpsimd.memset(ones[:], 1.0).then_inc(s_const, 1)
                pool.wait_ge(s_zero, 1)
                nc.gpsimd.memset(zeros.bitcast(I32)[:, H:H + 1], N_NODES).then_inc(s_zero, 1)
                for ramp, first in ((iota1[:], 1), (iota1b[:], 1), (iota1h[:], 1), (iota_t[:], 0)):
                    nc.gpsimd.iota(ramp, [[1, ramp.shape[1]]], base=first, channel_multiplier=0,
                                   allow_small_or_imprecise_dtypes=True).then_inc(s_const, 1)
                nc.gpsimd.iota(pwork["tile_id"], [[1, 7]], base=0, channel_multiplier=7, allow_small_or_imprecise_dtypes=True).then_inc(s_const, 1)
                for col, first, per_col, step in ((lane, 0, 1, 1), (no_row, P * SLOTS, P, 1), (first_row, -1 - P * SLOTS, -P, SLOTS - 1)):
                    nc.gpsimd.iota(col, [[per_col, col.shape[1]]], base=first, channel_multiplier=step, allow_small_or_imprecise_dtypes=True).then_inc(s_const, 1)
                pool.wait_ge(s_const, 10)
                nc.gpsimd.affine_select(out=ident[:], in_=ident[:], compare_op=ALU.not_equal, fill=1.0, base=0,
                                        pattern=[[-1, P]], channel_multiplier=1).then_inc(s_const, 1)
                nc.gpsimd.affine_select(out=tri[:], in_=ones[:], compare_op=ALU.is_gt, fill=0.0, base=0,
                                        pattern=[[1, P]], channel_multiplier=-1).then_inc(s_const, 1)
                nc.gpsimd.affine_select(out=row0[:], in_=ones[:], compare_op=ALU.is_equal, fill=0.0, base=0,
                                        pattern=[[0, P]], channel_multiplier=1).then_inc(s_const, 1)
                pool.wait_ge(s_const, 13)
                nc.gpsimd.tensor_copy(identb[:], ident[:]).then_inc(s_const, 1)
                pool.wait_ge(s_zero, 2)
                pool.wait_ge(s_pad, 1)
                pool.wait_ge(s_tail0, 16)
                for b in range(BLOCKS + 1):
                    if b < BLOCKS:
                        nc.gpsimd.indirect_dma_start(rec_rows, bass.IndirectOffsetOnAxis(pad_i[:, b:b + 1], 0), zeros, None).then_inc(s_padded, 16)
                    if b < BLOCKS:
                        a = a_f[:, b % 4, :]
                        pool.wait_ge(s_ac, 2 * b + 2)
                        nc.gpsimd.tensor_tensor(a, a, aparts[:, b, 0, :], ALU.subtract).then_inc(s_r1, 1)
                    if b >= 1:
                        pool.wait_ge(s_am, b)
                        nc.gpsimd.tensor_tensor(aparts[:, b - 1, 2, :], a_f[:, (b - 1) % 4, :], aparts[:, b - 1, 1, :],
                                                ALU.subtract).then_inc(s_sp, 1)
                pool.wait_ge(s_padded, 16 * BLOCKS)

            @block.scalar
            def _(act):
                pa(act)
                act.wait_ge(s_wt, 1)
                nc.scalar.activation(wabT, bank(4), ACT.Copy).then_inc(s_we, 1)
                nc.scalar.activation(weT[:], bank(5)[:, 0:Z], ACT.Copy).then_inc(s_we, 1)

                def xt(b):
                    act.wait_ge(s_xt, b + 1)
                    if b >= 2:
                        act.wait_ge(s_ab, b - 1)
                    nc.scalar.activation(xT[:, b % 2, :], bank(6)[:, 0:P], ACT.Copy).then_inc(s_xe, 1)

                xt(0)
                for b in range(BLOCKS + 1):
                    if b + 1 < BLOCKS:
                        xt(b + 1)
                    if b < BLOCKS:
                        act.wait_ge(s_ab, b + 1)
                        nc.scalar.activation(aparts[:, b, 0, :], bank(4 + b % 2)[:, 0:Z], ACT.Copy).then_inc(s_ac, 1)
                        if b >= 4:
                            act.wait_ge(s_sp, b - 3)
                            act.wait_ge(s_bst[b % 4], 16 * (b // 4))
                        nc.scalar.activation(a_f[:, b % 4, :], bank(4 + b % 2)[:, 0:Z], ACT.Copy).then_inc(s_ac, 1)
                        nc.scalar.activation(b_f[:, b % 4, :], bank(4 + b % 2)[:, Z:2 * Z], ACT.Copy).then_inc(s_bc, 1)
                    if b >= 1:
                        act.wait_ge(s_r1, b)
                        nc.scalar.activation(aparts[:, b - 1, 1, :], a_f[:, (b - 1) % 4, :], ACT.Copy).then_inc(s_am, 1)
                        act.wait_ge(s_bc, b)
                        act.dma_start(b_tab[(b - 1) * P:b * P, :], b_f[:, (b - 1) % 4, :]).then_inc(s_bst[(b - 1) % 4], 16)
                for i in range(4):
                    act.wait_ge(s_bst[i], 16 * len(range(i, BLOCKS, 4)))

            @block.vector
            def _(dve):
                n = [0]

                def after(ins):
                    n[0] += 1
                    ins.then_inc(s_kc, 1)
                    dve.wait_ge(s_kc, n[0])

                dve.wait_ge(s_load, 64)
                after(nc.vector.tensor_scalar(hi_i, src_i, 7, None, ALU.logical_shift_right))
                after(nc.vector.tensor_copy(hi, hi_i))
                after(nc.vector.tensor_scalar(pos_i, src_i, P - 1, None, ALU.bitwise_and))
                dve.wait_ge(s_const, N_CONST)
                pv(dve)
                after(nc.vector.tensor_scalar(loc1, pos_i, 1.0, None, ALU.add))
                after(nc.vector.tensor_copy(pos_i, pos))
                after(nc.vector.tensor_scalar(hi_i, pos_i, P - 1, None, ALU.bitwise_and))
                after(nc.vector.tensor_scalar(pos_i, pos_i, 7, None, ALU.logical_shift_right))
                after(nc.vector.tensor_copy(hi, pos_i))
                after(nc.vector.scalar_tensor_tensor(pos, hi_i, float(SLOTS), hi, ALU.mult, ALU.add))
                after(nc.vector.tensor_copy(row_i, pos))

            @block.tensor
            def _(pe):
                pe.wait_ge(s_w, 32)
                pe.wait_ge(s_const, N_CONST)
                for h in range(2):
                    for part, dest in ((0, bank(4)[:, h * P:(h + 1) * P]), (1, bank(4)[:, Z + h * P:Z + (h + 1) * P]),
                                       (2, bank(5)[:, h * P:(h + 1) * P])):
                        last = nc.tensor.transpose(dest, w_sb[:, h, part * H:(part + 1) * H], ident[:])
                last.then_inc(s_wt, 1)
                pt(pe)
                pe.wait_ge(s_x, 32)
                pe.wait_ge(s_we, 2)

                def transpose(b):
                    if b >= 1:
                        pe.wait_ge(s_xe, b)
                    nc.tensor.transpose(bank(6)[:, 0:P], x_sb[:, b, :], ident[:]).then_inc(s_xt, 1)

                transpose(0)
                for b in range(BLOCKS):
                    if b + 1 < BLOCKS:
                        transpose(b + 1)
                    pe.wait_ge(s_xe, b + 1)
                    if b >= 2:
                        pe.wait_ge(s_bc, b - 1)
                    nc.tensor.matmul(bank(4 + b % 2), xT[:, b % 2, :], wabT, start=True, stop=False)
                    nc.tensor.matmul(bank(4 + b % 2)[:, 0:Z], row0[:], bias_bc, start=False, stop=True).then_inc(s_ab, 1)

        fresh(EARLY)
        e_buf = tmp([2, G_IN, REC], F32)
        e_idx = tmp([2, G_IN], I32)
        t_buf = tmp([REC], F32)
        HOTS = 5
        hot_tile = tmp([HOTS, SLOTS], F16)
        hi2 = tmp([T_ALL + 1], F16)[:, 0:T_ALL]
        pos2 = tmp([T_ALL], F32)
        pos_i2 = tmp([T_ALL], I32)
        pos_j2 = tmp([T_ALL], I32)
        ring_at = cursor[0]
        h_ring2 = tmp([4, T_ALL + 1], BF16)[:, :, 0:T_ALL]
        ring_end = cursor[0]
        fresh(ring_at)
        hot_lane = tmp([HOTS, 2, P], F16)
        assert cursor[0] <= ring_end
        fresh(ring_end)
        cnt2 = tmp([BLOCKS], F32)
        offs2 = tmp([BLOCKS], F32)
        pwork2 = place_work(False)
        l_a = tmp([SLOTS], F32)
        l_b = tmp([SLOTS], I32)
        l_c = tmp([SLOTS], I32)
        assert cursor[0] <= APARTS_AT, (cursor[0], APARTS_AT)
        s_kc2, s_const2 = sem("key_chain2"), sem("const2")
        pv2, _, pt2, ps2 = place_steps("bydst", hi2, pos2, cnt2, offs2, h_ring2, pwork2, False)
        s_el = [sem(f"edges_loaded{i}") for i in range(2)]
        s_er = [sem(f"rows_ready{i}") for i in range(2)]
        s_es = [sem(f"rows_scattered{i}") for i in range(2)]
        s_tl, s_tr, s_ts = sem("tail_loaded"), sem("tail_ready"), sem("tail_scattered")
        s_hot, s_list = sem("one_hots"), sem("list_product")
        edge_in = edge[0:P * T_IN, :].rearrange("(p t) f -> p t f", p=P)
        UL = 10
        assert T_IN % UL == 0 and UL % HOTS == 0 and N_NODES < ROWS

        with nc.Block() as block:
            @block.sync
            def _(sp):
                sp.dma_start(t_buf[0:TAIL, 0:H], edge[P * T_IN:N_EDGES, :]).then_inc(s_tl, 16)

                def load(g, s):
                    sp.dma_start(e_buf[:, s, :, 0:H], edge_in[:, bass.ds(g * G_IN, G_IN), :]).then_inc(s_el[s], 16)

                load(0, 0)
                load(1, 1)
                with sp.Fori(1, N_GROUPS_IN // 2) as it:
                    for s in range(2):
                        sp.wait_ge(s_es[s], it * (16 * G_IN))
                        settle(sp, s_sp_turn)
                        load(2 * it + s, s)
                sp.wait_ge(s_es[0], (N_GROUPS_IN // 2) * 16 * G_IN)
                load(N_GROUPS_IN - 1, 0)
                ps2(sp, 1)

            @block.scalar
            def _(act):
                def fill(g, s):
                    cols = bass.ds(g * G_IN, G_IN)
                    nc.scalar.activation(e_buf[:, s, :, H:H + 1].bitcast(I32).rearrange("p g a -> p (g a)"), dst_i[:, cols], ACT.Copy).then_inc(s_er[s], 1)
                    nc.scalar.activation(e_buf[:, s, :, H + 1:H + 2].rearrange("p g a -> p (g a)"), loc1[:, cols], ACT.Copy).then_inc(s_er[s], 1)
                    nc.scalar.activation(e_idx[:, s, :], row_i[:, cols], ACT.Copy).then_inc(s_er[s], 1)

                nc.scalar.activation(t_buf[:, H:H + 1].bitcast(I32), dst_i[:, T_IN:T_ALL], ACT.Copy).then_inc(s_tr, 1)
                nc.scalar.activation(t_buf[:, H + 1:H + 2], loc1[:, T_IN:T_ALL], ACT.Copy).then_inc(s_tr, 1)
                fill(0, 0)
                fill(1, 1)
                with act.Fori(1, N_GROUPS_IN // 2) as it:
                    for s in range(2):
                        act.wait_ge(s_es[s], it * (16 * G_IN))
                        fill(2 * it + s, s)
                act.wait_ge(s_es[0], (N_GROUPS_IN // 2) * 16 * G_IN)
                fill(N_GROUPS_IN - 1, 0)

            @block.gpsimd
            def _(pool):
                nc.gpsimd.iota(pwork2["tile_id"], [[1, 7]], base=0, channel_multiplier=7, allow_small_or_imprecise_dtypes=True).then_inc(s_const2, 1)

                def scatter(it1, s):
                    pool.wait_ge(s_el[s], it1 * 16)
                    pool.wait_ge(s_er[s], it1 * 3)
                    settle(pool, s_turn)
                    for k in range(G_IN):
                        nc.gpsimd.indirect_dma_start(rec_rows, bass.IndirectOffsetOnAxis(e_idx[:, s, k:k + 1], 0),
                                                     e_buf[:, s, k, :], None).then_inc(s_es[s], 16)

                pool.wait_ge(s_tl, 16)
                pool.wait_ge(s_tr, 2)
                nc.gpsimd.indirect_dma_start(rec_rows, bass.IndirectOffsetOnAxis(row_i[0:TAIL, T_IN:T_ALL], 0),
                                             t_buf[0:TAIL, :], None).then_inc(s_ts, 16)
                with pool.Fori(0, N_GROUPS_IN // 2) as it:
                    for s in range(2):
                        scatter(it + 1, s)
                scatter(N_GROUPS_IN // 2 + 1, 0)
                pool.wait_ge(s_es[0], (N_GROUPS_IN // 2 + 1) * 16 * G_IN)
                pool.wait_ge(s_es[1], (N_GROUPS_IN // 2) * 16 * G_IN)
                pool.wait_ge(s_ts, 16)

            @block.vector
            def _(dve):
                n = [0]

                def after(ins):
                    n[0] += 1
                    ins.then_inc(s_kc2, 1)
                    dve.wait_ge(s_kc2, n[0])

                after(nc.vector.tensor_scalar(pos_i2, dst_i, 7, None, ALU.logical_shift_right))
                after(nc.vector.tensor_copy(hi2, pos_i2))
                dve.wait_ge(s_const2, 1)
                pv2(dve)
                after(nc.vector.tensor_copy(pos_i2, pos2))
                after(nc.vector.tensor_scalar(pos_j2, pos_i2, P - 1, None, ALU.bitwise_and))
                after(nc.vector.tensor_scalar(lane_f, pos_j2, 1.0, None, ALU.add))
                after(nc.vector.tensor_scalar(pos_i2, pos_i2, 7, None, ALU.logical_shift_right))
                after(nc.vector.tensor_copy(tile_f, pos_i2))
                after(nc.vector.tensor_scalar(hi2[:, T_IN:T_ALL], hi2[:, T_IN:T_ALL], 64.0, 4096.0, ALU.is_ge, ALU.mult))
                after(nc.vector.tensor_tensor(tile_f[:, T_IN:T_ALL], tile_f[:, T_IN:T_ALL], hi2[:, T_IN:T_ALL], ALU.add))
                after(nc.vector.tensor_scalar(pos_i2, src_i, 2, None, ALU.logical_shift_right))
                after(nc.vector.tensor_copy(v_a, pos_i2))
                after(nc.vector.tensor_scalar(pos_i2, src_i, 3, None, ALU.bitwise_and))
                after(nc.vector.tensor_scalar(pos_j2, dst_i, P - 1, None, ALU.bitwise_and))
                after(nc.vector.tensor_scalar(pos2, pos_i2, 256.0, 1.0, ALU.mult, ALU.add))
                after(nc.vector.tensor_tensor(v_b, pos2, pos_j2, ALU.add))

                def hots(t, s, used):
                    if used is not None:
                        dve.wait_ge(s_list, used)
                    col = bass.ds(t, 1)
                    nc.vector.tensor_scalar(hot_tile[:, s, :], iota_t[:], tile_f[:, col], None, ALU.is_equal)
                    for k, v in enumerate((v_a, v_b)):
                        last = nc.vector.tensor_scalar(hot_lane[:, s, k, :], iota1h[:], lane_f[:, col], v[:, col], ALU.is_equal, ALU.mult)
                    last.then_inc(s_hot, 1)

                for t in range(UL):
                    hots(t, t % HOTS, t + 1 - HOTS if t >= HOTS else None)
                with dve.Fori(1, T_IN // UL) as it:
                    for k in range(UL):
                        hots(it * UL + k, k % HOTS, it * UL + (k + 1 - HOTS))
                hots(T_IN, T_IN % HOTS, T_ALL - HOTS)
                dve.wait_ge(s_list, T_ALL)
                both = psum[:, 4:8, 0:HALF]
                after(nc.vector.tensor_copy(l_a.rearrange("p (a n) -> p a n", a=2), both[:, 0:2, :]))
                after(nc.vector.tensor_copy(l_b.rearrange("p (a n) -> p a n", a=2), both[:, 2:4, :]))
                after(nc.vector.tensor_scalar(l_c, l_b, 255, None, ALU.bitwise_and))
                after(nc.vector.tensor_copy(l1_loc[:], l_c))
                after(nc.vector.tensor_scalar(l_c, l_b, 8, None, ALU.logical_shift_right))
                after(nc.vector.scalar_tensor_tensor(l1_idx[:], l_a, 4.0, l_c, ALU.mult, ALU.add))

            @block.tensor
            def _(pe):
                pt2(pe)

                def product(t1, s, start, stop):
                    pe.wait_ge(s_hot, t1)
                    for k in range(2):
                        for h in range(2):
                            last = nc.tensor.matmul(bank(4 + 2 * k + h)[:, 0:HALF], hot_lane[:, s, k, :],
                                                    hot_tile[:, s, h * HALF:(h + 1) * HALF], start=start, stop=stop)
                    last.then_inc(s_list, 1)

                for t in range(UL):
                    product(t + 1, t % HOTS, t == 0, False)
                with pe.Fori(1, T_IN // UL) as it:
                    for k in range(UL):
                        product(it * UL + (k + 1), k % HOTS, False, False)
                product(T_ALL, T_IN % HOTS, False, True)

        fresh()
        YG, YS = 4, 4
        Y_GROUPS = SLOTS // YG
        rec = tmp([YS, YG, REC], F32)
        bg = tmp([YS, YG, Z], F32)
        zb = tmp([YS, YG, Z], F32)
        hot = tmp([YS, YG, P], BF16)
        hotT = tmp([YS, YG, P], BF16)
        eT = tmp([YS, YG, P], F32)
        acc = tmp([2, 2 * Z], F32)
        assert cursor[0] <= APARTS_AT, (cursor[0], APARTS_AT)
        s_rl = [sem(f"rec_loaded{i}") for i in range(YS)]
        s_bg = [sem(f"b_gathered{i}") for i in range(YS)]
        s_zs = [sem(f"z_stored{i}") for i in range(YS)]
        s_oh, s_oht, s_ohe, s_et, s_ee = sem("hot"), sem("hot_transposed"), sem("hotT_copied"), sem("e_transposed"), sem("eT_copied")
        s_zp, s_za, s_sq, s_acc, s_accz, s_sl = sem("z_product"), sem("z_added"), sem("z_squared"), sem("squares_added"), sem("z_accumulated"), sem("srcloc_copied")
        s_fin, s_fc, s_gb = sem("sums_done"), sem("stat_chain"), sem("gamma_loaded")
        acc_z = bank(7)
        sums = bank(0)

        with nc.Block() as block:
            @block.sync
            def _(sp):
                with nc.allow_non_contiguous_dma(reason="two short vectors, once"):
                    sp.dma_start(stat[:, 4:6], gamma0.rearrange("(h p) -> p h", p=P)).then_inc(s_gb, 16)
                    sp.dma_start(stat[:, 6:8], beta0.rearrange("(h p) -> p h", p=P)).then_inc(s_gb, 16)

                def load(g, s, use):
                    wait(sp, s_bg[s], (use - 1) * (16 * YG))
                    settle(sp, s_sp_turn)
                    for done in (s_sl, s_oh, s_et):
                        wait(sp, done, g - 3)
                        settle(sp, s_sp_turn)
                    sp.dma_start(rec[:, s, :, :], rec_d[:, bass.ds(g * YG, YG), :]).then_inc(s_rl[s], 16)

                groups(sp, load, None, Y_GROUPS, YS)

            @block.gpsimd
            def _(pool):
                def gather(g, s, use):
                    wait(pool, s_rl[s], use * 16)
                    wait(pool, s_za, 2 * g - 6)
                    settle(pool, s_turn)
                    for k in range(YG):
                        nc.gpsimd.indirect_dma_start(bg[:, s, k, :], None, b_tab,
                                                     bass.IndirectOffsetOnAxis(rec[:, s, k, H:H + 1].bitcast(I32), 0)).then_inc(s_bg[s], 16)

                groups(pool, gather, None, Y_GROUPS, YS)
                for s in range(YS):
                    pool.wait_ge(s_bg[s], (Y_GROUPS // YS) * 16 * YG)

            @block.vector
            def _(dve):
                def hots(g, s, use):
                    wait(dve, s_rl[s], use * 16)
                    wait(dve, s_oht, g - 3)
                    for k in range(YG):
                        last = nc.vector.tensor_scalar(hot[:, s, k, :], iota1b[:], rec[:, s, k, H + 1:H + 2], None, ALU.is_equal)
                    last.then_inc(s_oh, 1)

                def add(g, s, use):
                    wait(dve, s_bg[s], use * (16 * YG))
                    wait(dve, s_zs[s], (use - 1) * 16)
                    for q in range(2):
                        wait(dve, s_zp, 2 * g + (q + 1))
                        nc.vector.tensor_tensor(zb[:, s, 2 * q:2 * q + 2, :].rearrange("p a z -> p (a z)"), bank(3 + q % 2),
                                                bg[:, s, 2 * q:2 * q + 2, :].rearrange("p a z -> p (a z)"), ALU.add).then_inc(s_za, 1)
                        if q >= 1 or not (isinstance(g, int) and g == 0):
                            accumulate(2 * g + (q - 1), 1 - q)
                        wait(dve, s_za, 2 * g + (q + 1))
                        wait(dve, s_accz, 2 * g + (q + 1))
                        nc.vector.tensor_tensor(acc_z, zb[:, s, 2 * q:2 * q + 2, :].rearrange("p a z -> p (a z)"), acc_z, ALU.add).then_inc(s_accz, 1)

                def accumulate(n, b):
                    wait(dve, s_sq, n + 1)
                    wait(dve, s_acc, n + 1)
                    nc.vector.tensor_tensor(acc[:, 0, :], bank(5 + b), acc[:, 0, :], ALU.add).then_inc(s_acc, 1)

                nc.vector.memset(acc[:, 0, :], 0.0).then_inc(s_acc, 1)
                nc.vector.memset(acc_z, 0.0).then_inc(s_accz, 1)
                groups(dve, hots, add, Y_GROUPS, YS, lag=2)
                accumulate(2 * Y_GROUPS - 1, 1)
                dve.wait_ge(s_accz, 2 * Y_GROUPS + 1)
                nc.vector.tensor_copy(acc[:, 1, :], acc_z).then_inc(s_accz, 1)
                n = [0]

                def after(ins):
                    n[0] += 1
                    ins.then_inc(s_fc, 1)
                    dve.wait_ge(s_fc, n[0])

                dve.wait_ge(s_gb, 32)
                dve.wait_ge(s_fin, 1)
                mean, ex2, var = stat[:, 8:10], stat[:, 10:12], stat[:, 12:14]
                after(nc.vector.tensor_scalar(mean, sums[:, 0:2], 1.0 / N_EDGES, None, ALU.mult))
                after(nc.vector.tensor_scalar(ex2, sums[:, 2:4], 1.0 / N_EDGES, None, ALU.mult))
                after(nc.vector.tensor_tensor(var, mean, mean, ALU.mult))
                after(nc.vector.tensor_tensor(var, ex2, var, ALU.subtract))
                after(nc.vector.tensor_scalar(var, var, 0.0, BN_EPS, ALU.max, ALU.add))
                dve.wait_ge(s_fin, 2)
                after(nc.vector.reciprocal(ex2, var))
                after(nc.vector.tensor_tensor(bn_s, ex2, stat[:, 4:6], ALU.mult))
                after(nc.vector.tensor_tensor(mean, mean, bn_s, ALU.mult))
                after(nc.vector.tensor_tensor(bn_t, stat[:, 6:8], mean, ALU.subtract))
                after(nc.vector.tensor_scalar(stat[:, 4:5], bn_s[:, 0:1], -1.0, None, ALU.mult))
                after(nc.vector.tensor_scalar(stat[:, 5:6], bn_t[:, 0:1], -1.0, None, ALU.mult))

            @block.scalar
            def _(act):
                def copies(g, s, use):
                    wait(act, s_rl[s], use * 16)
                    nc.scalar.activation(srcloc[:, bass.ds(g * YG, YG)], rec[:, s, :, H + 1:H + 2].rearrange("p g a -> p (g a)"), ACT.Copy).then_inc(s_sl, 1)
                    wait(act, s_oht, g + 1)
                    wait(act, s_zp, 2 * g - 6)
                    nc.scalar.activation(hotT[:, s, :, :].rearrange("p g n -> p (g n)"), bank(0).bitcast(BF16)[:, 0:YG * P], ACT.Copy).then_inc(s_ohe, 1)
                    wait(act, s_et, g + 1)
                    nc.scalar.activation(eT[:, s, :, :].rearrange("p g n -> p (g n)"), bank(1 + s % 2), ACT.Copy).then_inc(s_ee, 1)

                def square(g, s, use):
                    for q in range(2):
                        wait(act, s_za, 2 * g + (q + 1))
                        wait(act, s_acc, 2 * g + q)
                        nc.scalar.activation(bank(5 + q % 2), zb[:, s, 2 * q:2 * q + 2, :].rearrange("p a z -> p (a z)"), ACT.Square).then_inc(s_sq, 1)
                    act.dma_start(z_d[:, bass.ds(g * YG, YG), :], zb[:, s, :, :]).then_inc(s_zs[s], 16)

                groups(act, copies, square, Y_GROUPS, YS, lag=2)
                for s in range(YS):
                    act.wait_ge(s_zs[s], (Y_GROUPS // YS) * 16)
                act.wait_ge(s_fc, 5)
                nc.scalar.activation(stat[:, 12:14], stat[:, 12:14], ACT.Sqrt).then_inc(s_fin, 1)

            @block.tensor
            def _(pe):
                def transposes(g, s, use):
                    wait(pe, s_oh, g + 1)
                    wait(pe, s_ohe, g)
                    for k in range(YG):
                        last = nc.tensor.transpose(bank(0).bitcast(BF16)[:, k * P:(k + 1) * P], hot[:, s, k, :], identb[:])
                    last.then_inc(s_oht, 1)
                    wait(pe, s_rl[s], use * 16)
                    wait(pe, s_ee, g - 1)
                    for k in range(YG):
                        last = nc.tensor.transpose(bank(1 + s % 2)[:, k * P:(k + 1) * P], rec[:, s, k, 0:H], ident[:])
                    last.then_inc(s_et, 1)

                def product(g, s, use):
                    _, blocks = nc.values_load_multi_w_load_instructions(
                        blk_row[0:1, 0, bass.ds(g * YG, YG)], engines=[PE_ENGINE], min_val=0, max_val=BLOCKS - 1,
                        skip_runtime_bounds_check_because="the ids are clamped when made")
                    wait(pe, s_ohe, g + 1)
                    wait(pe, s_ee, g + 1)
                    for q in range(2):
                        wait(pe, s_za, 2 * g + (q - 1))
                        for a in range(2):
                            k = 2 * q + a
                            zp = bank(3 + q % 2)[:, a * Z:(a + 1) * Z]
                            nc.tensor.matmul(zp, eT[:, s, k, :], weT[:], start=True, stop=False)
                            for part in range(3):
                                rhs = aparts[:, bass.ds(blocks[k], 1), part, :].rearrange("p a z -> p (a z)")
                                last = nc.tensor.matmul(zp, hotT[:, s, k, :], rhs, start=False, stop=(part == 2))
                        last.then_inc(s_zp, 1)

                groups(pe, transposes, product, Y_GROUPS, YS)
                pe.wait_ge(s_acc, 2 * Y_GROUPS + 1)
                pe.wait_ge(s_accz, 2 * Y_GROUPS + 2)
                pe.wait_ge(s_ohe, Y_GROUPS)
                for h in range(2):
                    for col, which in ((h, 1), (2 + h, 0)):
                        for a in range(2):
                            last = nc.tensor.matmul(sums[:, col:col + 1], acc[:, which, a * Z + h * H:a * Z + (h + 1) * H], ones[:, 0:1],
                                                    start=(a == 0), stop=(a == 1))
                last.then_inc(s_fin, 1)

        AT_EXP, AT_HOLD, AT_LOG, AT_MAX, AT_MULT, AT_BACK, AT_COPY, AT_SUM, AT_ADD = range(1, 10)
        fresh()
        zl = tmp([2, G, Z], F32)
        hotf = tmp([4, 4, P], F32)
        vaf, sig = tmp([4, 4 * P], F32), tmp([4, 4 * P], F32)
        spl, mT, msg = (tmp([2, 4 * P], F32) for _ in range(3))
        ex = tmp([4, 8 * P], F32)
        agg_at = cursor[0]
        agg = tmp([2, BLOCKS, H], F32)
        N_HALVES = 2 * N_GROUPS
        EXP_MAX = 2.0 ** 62
        LOG, BACK, SUMS = 4, 6, 7
        s_zl = [sem(f"z_loaded{i}") for i in range(2)]
        (s_hf, s_zt, s_ex, s_va, s_cl, s_lg, s_sig, s_spl, s_msgT, s_mt, s_mc, s_sc, s_fl) = (
            sem(n) for n in ("hot32", "z_transposed", "exps", "v_scaled", "exps_held", "logs", "sigmoid",
                             "softplus", "messageT", "message_transposed", "message_copied", "segment_product", "segment_added"))

        def halves(eng, step, lag):
            for m in range(12):
                step(m, m % 4, m // 4)
            with eng.Fori(3, N_HALVES // 4) as it:
                for j in range(4):
                    step(4 * it + j, j, it)
            for m in range(N_HALVES, N_HALVES + lag):
                step(m, m % 4, m // 4)

        def there(n):
            return not isinstance(n, int) or 0 <= n < N_HALVES

        with nc.Block() as block:
            @block.sync
            def _(sp):
                def load(g, s, use):
                    wait(sp, s_zt, 2 * g - 2)
                    settle(sp, s_sp_turn)
                    sp.dma_start(zl[:, s, :, :], z_d[:, bass.ds(g * G, G), :]).then_inc(s_zl[s], 16)

                groups(sp, load, None, N_GROUPS, 2)

            @block.tensor
            def _(pe):
                def step(m, j, it):
                    if there(m):
                        h, s = j % 2, j // 2
                        wait(pe, s_zl[s], it * 16 + 16)
                        wait(pe, s_ex, 2 * m - 2)
                        wait(pe, s_va, m - 1)
                        for part in range(2):
                            for k in range(4):
                                last = nc.tensor.transpose(bank(2 * h + 1 - part)[:, k * P:(k + 1) * P],
                                                           zl[:, s, 4 * h + k, part * H:(part + 1) * H], ident[:])
                        last.then_inc(s_zt, 1)
                    n, h = m - AT_BACK, (j - AT_BACK) % 2
                    if there(n):
                        wait(pe, s_msgT, n + 1)
                        wait(pe, s_mc, n)
                        for k in range(4):
                            last = nc.tensor.transpose(bank(BACK)[:, k * P:(k + 1) * P], mT[:, h, k * P:(k + 1) * P], ident[:])
                        last.then_inc(s_mt, 1)
                    n, h, r = m - AT_SUM, (j - AT_SUM) % 2, (j - AT_SUM) % 4
                    if there(n):
                        wait(pe, s_mc, n + 1)
                        wait(pe, s_hf, n + 1)
                        wait(pe, s_fl, 4 * n + 2)
                        for k in range(4):
                            last = nc.tensor.matmul(bank(SUMS)[:, k * P:(k + 1) * P], hotf[:, r, k, :],
                                                    msg[:, h, k * P:(k + 1) * P], start=True, stop=True)
                        last.then_inc(s_sc, 1)

                halves(pe, step, AT_SUM)

            @block.scalar
            def _(act):
                def step(m, j, it):
                    n, h, r = m - AT_EXP, (j - AT_EXP) % 2, (j - AT_EXP) % 4
                    if there(n):
                        wait(act, s_zt, n + 1)
                        wait(act, s_lg, n - 3)
                        nc.scalar.activation(ex[:, r, 0:4 * P], bank(2 * h), ACT.Exp, bias=bn_t[:, 1:2], scale=bn_s[:, 1:2]).then_inc(s_ex, 1)
                        nc.scalar.activation(ex[:, r, 4 * P:8 * P], bank(2 * h + 1), ACT.Exp, bias=stat[:, 5:6], scale=stat[:, 4:5]).then_inc(s_ex, 1)
                        wait(act, s_spl, n - 3)
                        nc.scalar.activation(vaf[:, r, :], bank(2 * h), ACT.Identity, bias=bn_t[:, 1:2], scale=bn_s[:, 1:2]).then_inc(s_va, 1)
                    n, r = m - AT_LOG, (j - AT_LOG) % 4
                    if there(n):
                        wait(act, s_cl, n + 1)
                        wait(act, s_spl, n)
                        wait(act, s_sig, n)
                        nc.scalar.activation(psum[:, LOG:LOG + 2, :].rearrange("p a n -> p (a n)"), ex[:, r, :], ACT.Ln, bias=1.0).then_inc(s_lg, 1)
                        wait(act, s_lg, n + 1)
                        wait(act, s_msgT, n - 3)
                        nc.scalar.activation(sig[:, r, :], bank(LOG + 1), ACT.Exp, scale=-1.0).then_inc(s_sig, 1)

                act.preload_act_table_set("natural_log_exp_and_others")
                halves(act, step, AT_LOG)

            @block.gpsimd
            def _(pool):
                def step(m, j, it):
                    n, h, r = m - AT_MULT, (j - AT_MULT) % 2, (j - AT_MULT) % 4
                    if there(n):
                        wait(pool, s_spl, n + 1)
                        wait(pool, s_sig, n + 1)
                        wait(pool, s_mt, n - 1)
                        nc.gpsimd.tensor_tensor(mT[:, h, :], spl[:, h, :], sig[:, r, :], ALU.mult).then_inc(s_msgT, 1)

                halves(pool, step, AT_MULT)

            @block.vector
            def _(dve):
                def step(m, j, it):
                    n, h, r = m - AT_MAX, (j - AT_MAX) % 2, (j - AT_MAX) % 4
                    if there(n):
                        wait(dve, s_lg, n + 1)
                        wait(dve, s_va, n + 1)
                        wait(dve, s_msgT, n - 1)
                        nc.vector.tensor_tensor(spl[:, h, :], bank(LOG), vaf[:, r, :], ALU.max).then_inc(s_spl, 1)
                    n, h = m - AT_COPY, (j - AT_COPY) % 2
                    if there(n):
                        wait(dve, s_mt, n + 1)
                        wait(dve, s_sc, n - 1)
                        nc.vector.tensor_copy(msg[:, h, :], bank(BACK)).then_inc(s_mc, 1)
                    n = m - AT_ADD
                    if there(n):
                        _, blocks = nc.values_load_multi_w_load_instructions(
                            blk_row[0:1, 0, bass.ds(n * 4, 4)], engines=[DVE_ENGINE], min_val=0, max_val=BLOCKS - 1,
                            skip_runtime_bounds_check_because="the ids are clamped when made")
                        wait(dve, s_sc, n + 1)
                        for k in range(4):
                            wait(dve, s_fl, 4 * n + (k - 1) + 2)
                            dest = agg[:, k % 2, bass.ds(blocks[k], 1), :].rearrange("p a f -> p (a f)")
                            nc.vector.tensor_tensor(dest, bank(SUMS)[:, k * P:(k + 1) * P], dest, ALU.add).then_inc(s_fl, 1)
                    n, r = m - AT_HOLD, (j - AT_HOLD) % 4
                    if there(n):
                        wait(dve, s_ex, 2 * n + 2)
                        nc.vector.tensor_scalar(ex[:, r, :], ex[:, r, :], EXP_MAX, None, ALU.min).then_inc(s_cl, 1)
                    n, r = m - AT_COPY, (j - AT_COPY) % 4
                    if there(n):
                        wait(dve, s_sc, n - 3)
                        for k in range(4):
                            col = srcloc[:, n * 4 + k:n * 4 + k + 1] if isinstance(n, int) else srcloc[:, bass.ds(n * 4 + k, 1)]
                            last = nc.vector.tensor_scalar(hotf[:, r, k, :], iota1[:], col, None, ALU.is_equal)
                        last.then_inc(s_hf, 1)

                nc.vector.tensor_scalar(agg[:, 0, :, :].rearrange("p b f -> p (b f)"), x_sb[:].rearrange("p b f -> p (b f)"),
                                        2.0, None, ALU.mult).then_inc(s_fl, 1)
                nc.vector.memset(agg[:, 1, :, :], 0.0).then_inc(s_fl, 1)
                halves(dve, step, AT_ADD)

        x1 = tmp([BLOCKS, H + 1], F32)
        red = tmp([8, BLOCKS], F32)
        s_n, s_nq, s_xs = sem("norm0_chain"), sem("norm0_root"), sem("x1_stored")

        def bc(v):
            return v.unsqueeze(2).broadcast_to([P, BLOCKS, H])

        PARTS = [slice(0, 24), slice(24, BLOCKS)]

        def layernorm(after, squares, root, y, scr, dest, written=None):
            mean, var, rs = red[:, 0, :], red[:, 1, :], red[:, 2, :]
            after(nc.vector.tensor_reduce(mean, y, op=ALU.add, axis=AX_X))
            after(nc.vector.tensor_scalar(mean, mean, 1.0 / H, None, ALU.mult))
            for part in PARTS:
                n = part.stop - part.start
                squares.ask(nc.vector.tensor_tensor(y[:, part, :], y[:, part, :], mean[:, part].unsqueeze(2).broadcast_to([P, n, H]), ALU.subtract))
            for part in PARTS:
                squares.wait()
                last = nc.vector.tensor_reduce(var[:, part], scr[:, part, :], op=ALU.add, axis=AX_X)
            after(last)
            after(nc.vector.tensor_scalar(var, var, 1.0 / H, LN_EPS, ALU.mult, ALU.add))
            root()
            after(nc.vector.reciprocal(rs, var))
            if written is None:
                after(nc.vector.tensor_tensor(dest, y, bc(rs), ALU.mult))
                return
            for part in PARTS:
                n = part.stop - part.start
                nc.vector.tensor_tensor(dest[:, part, :], y[:, part, :], rs[:, part].unsqueeze(2).broadcast_to([P, n, H]),
                                        ALU.mult).then_inc(written, 1)

        class Squares:

            def __init__(self, tag):
                self.asked, self.made, self.n, self.m = sem(f"{tag}_square_asked"), sem(f"{tag}_squared"), 0, 0

            def ask(self, instruction):
                instruction.then_inc(self.asked, 1)

            def wait(self):
                self.n += 1
                nc.vector.wait_ge(self.made, self.n)

            def make(self, y, scr):
                for part in PARTS:
                    self.m += 1
                    nc.scalar.wait_ge(self.asked, self.m)
                    nc.scalar.activation(scr[:, part, :], y[:, part, :], ACT.Square).then_inc(self.made, 1)

        squares = Squares("norm0")
        s_x1w, s_t1, s_t1c = sem("x1_written"), sem("x1_transposed"), sem("x1T_copied")
        CH = [(b, min(4, BLOCKS - b)) for b in range(0, BLOCKS, 4)]
        x1T = x_sb
        average_at = 2 * G * (H + 1) + 2 * G * P + 4 * G
        keep = cursor[0]
        fresh(average_at)
        agg1 = tmp([BLOCKS, H + 1], F32)
        assert cursor[0] <= agg_at, (cursor[0], agg_at)
        fresh(keep)
        s_clear = sem("averages_cleared")

        with nc.Block() as block:
            @block.gpsimd
            def _(pool):
                nc.gpsimd.memset(agg1.rearrange("p b f -> p (b f)"), 0.0).then_inc(s_clear, 1)

            @block.vector
            def _(dve):
                n = [0]

                def after(ins):
                    n[0] += 1
                    ins.then_inc(s_n, 1)
                    dve.wait_ge(s_n, n[0])

                def root():
                    dve.sem_inc(s_nq, 1)
                    dve.wait_ge(s_nq, 2)

                y = agg[:, 0, :, :]
                after(nc.vector.tensor_tensor(y, y, agg[:, 1, :, :], ALU.add))
                after(nc.vector.memset(x1[:, :, H:H + 1], 1.0))
                layernorm(after, squares, root, y, agg[:, 1, :, :], x1[:, :, 0:H], s_x1w)

            @block.scalar
            def _(act):
                squares.make(agg[:, 0, :, :], agg[:, 1, :, :])
                act.wait_ge(s_nq, 1)
                nc.scalar.activation(red[:, 1, :], red[:, 1, :], ACT.Sqrt).then_inc(s_nq, 1)
                for c, (b0, nb) in enumerate(CH):
                    act.wait_ge(s_t1, c + 1)
                    nc.scalar.activation(x1T[:, b0:b0 + nb, :].rearrange("p b n -> p (b n)"), bank(c % 2)[:, 0:nb * P], ACT.Copy).then_inc(s_t1c, 1)

            @block.tensor
            def _(pe):
                for c, (b0, nb) in enumerate(CH):
                    pe.wait_ge(s_x1w, 1 if b0 + nb <= PARTS[0].stop else 2)
                    if c >= 2:
                        pe.wait_ge(s_t1c, c - 1)
                    for k in range(nb):
                        last = nc.tensor.transpose(bank(c % 2)[:, k * P:(k + 1) * P], x1[:, b0 + k, 0:H], ident[:])
                    last.then_inc(s_t1, 1)

            @block.sync
            def _(sp):
                for i, part in enumerate(PARTS):
                    sp.wait_ge(s_x1w, i + 1)
                    sp.dma_start(x1_tab.rearrange("(b p) f -> p b f", p=P)[:, part, :], x1[:, part, :]).then_inc(s_xs, 16)
                sp.wait_ge(s_xs, 16 * len(PARTS))

        x1_at = cursor[0] - 8 * BLOCKS - BLOCKS * (H + 1)
        fresh()
        xg = tmp([2, G, H + 1], F32)
        hotg = tmp([2, G, P], F32)
        gi = tmp([2, G], I32)
        gl = tmp([2, G], F32)
        assert cursor[0] == average_at
        fresh(average_at + BLOCKS * (H + 1))
        enh = tmp([BLOCKS, H], F32)
        x1b = tmp([BLOCKS, H], F32)
        w1s = tmp([64], F32)
        w2s = tmp([H], F32)
        b1s = tmp([1], F32)
        gb = tmp([2, H], F32)
        s_wl = sem("w12_loaded")
        assert cursor[0] <= x1_at, (cursor[0], x1_at)
        s_xg = [sem(f"x1_gathered{i}") for i in range(2)]
        s_gi, s_hg, s_sg, s_fg = sem("list_columns"), sem("hot_by_dst"), sem("average_product"), sem("average_added")

        with nc.Block() as block:
            @block.sync
            def _(sp):
                sp.dma_start(w1s, W1).then_inc(s_wl, 16)
                sp.dma_start(w2s[0:64, :], W2).then_inc(s_wl, 16)
                sp.dma_start(w2s[64:65, :], b2.rearrange("(a n) -> a n", a=1)).then_inc(s_wl, 16)
                with nc.allow_non_contiguous_dma(reason="a column, once"):
                    sp.dma_start(b1s[0:64, :], b1.rearrange("(p a) -> p a", a=1)).then_inc(s_wl, 16)
                for i, v in enumerate((gamma1, beta1)):
                    sp.dma_start(gb[:, i, :], v.rearrange("(a n) -> a n", a=1).broadcast_to([P, H])).then_inc(s_wl, 16)
                sp.wait_ge(s_wl, 16 * 6)

            @block.scalar
            def _(act):
                def columns(g, s, use):
                    wait(act, s_xg[s], (use - 1) * (16 * G))
                    wait(act, s_hg, g - 1)
                    nc.scalar.activation(gi[:, s, :], l1_idx[:, bass.ds(g * G, G)], ACT.Copy).then_inc(s_gi, 1)
                    nc.scalar.activation(gl[:, s, :], l1_loc[:, bass.ds(g * G, G)], ACT.Copy).then_inc(s_gi, 1)

                groups(act, columns, None, N_GROUPS, 2)

            @block.gpsimd
            def _(pool):
                def gather(g, s, use):
                    wait(pool, s_gi, 2 * g + 2)
                    wait(pool, s_sg, 4 * g - 4)
                    settle(pool, s_turn)
                    for k in range(G):
                        nc.gpsimd.indirect_dma_start(xg[:, s, k, :], None, x1_tab, bass.IndirectOffsetOnAxis(gi[:, s, k:k + 1], 0)).then_inc(s_xg[s], 16)

                groups(pool, gather, None, N_GROUPS, 2)

            @block.tensor
            def _(pe):
                def product(g, s, use):
                    wait(pe, s_hg, g + 1)
                    wait(pe, s_xg[s], use * (16 * G))
                    for q in range(4):
                        wait(pe, s_fg, 8 * g - 16 + 2 * q + 3)
                        for a in range(2):
                            last = nc.tensor.matmul(bank(4 * s + q)[:, a * 256:a * 256 + H + 1], hotg[:, s, 2 * q + a, :], xg[:, s, 2 * q + a, :],
                                                    start=True, stop=True)
                        last.then_inc(s_sg, 1)

                groups(pe, product, None, N_GROUPS, 2)

            @block.vector
            def _(dve):
                def hots(g, s, use):
                    wait(dve, s_gi, 2 * g + 2)
                    wait(dve, s_sg, 4 * g - 4)
                    for k in range(G):
                        last = nc.vector.tensor_scalar(hotg[:, s, k, :], iota1[:], gl[:, s, k:k + 1], None, ALU.is_equal)
                    last.then_inc(s_hg, 1)

                def add(g, s, use):
                    _, blocks = nc.values_load_multi_w_load_instructions(
                        blk_row[0:1, 1, bass.ds(g * G, G)], engines=[DVE_ENGINE], min_val=0, max_val=BLOCKS - 1,
                        skip_runtime_bounds_check_because="the ids are clamped when made")
                    for q in range(4):
                        wait(dve, s_sg, 4 * g + (q + 1))
                        for a in range(2):
                            k = 2 * q + a
                            wait(dve, s_fg, 8 * g + (k + 1))
                            dest = agg1[:, bass.ds(blocks[k], 1), :].rearrange("p a f -> p (a f)")
                            nc.vector.tensor_tensor(dest, bank(4 * s + q)[:, a * 256:a * 256 + H + 1], dest, ALU.add).then_inc(s_fg, 1)

                dve.sem_inc(s_fg, 1)
                groups(dve, hots, add, N_GROUPS, 2)

        hT = tmp([2, 512], F32)
        assert cursor[0] <= x1_at
        s_m1, s_m1c, s_m2, s_m2c = (sem(n) for n in ("mlp1", "mlp1_relu", "mlp2", "mlp2_copied"))
        s_f, s_fq, s_fc2, s_out = sem("finish_chain"), sem("finish_asked"), sem("finish_root"), sem("out_stored")
        s_xb, s_h1, s_yw = sem("x1_and_beta"), sem("h_row_of_ones"), sem("output_written")
        squares = Squares("finish")

        def bcv(i):
            return gb[:, i, :].unsqueeze(1).broadcast_to([P, BLOCKS, H])


        with nc.Block() as block:
            @block.sync
            def _(sp):
                whole = out[0:(BLOCKS - 1) * P, :].rearrange("(b p) f -> p b f", p=P)
                sp.wait_ge(s_yw, 1)
                sp.dma_start(whole[:, PARTS[0], :], enh[:, PARTS[0], :]).then_inc(s_out, 16)
                sp.wait_ge(s_yw, 2)
                sp.dma_start(whole[:, PARTS[1].start:BLOCKS - 1, :], enh[:, PARTS[1].start:BLOCKS - 1, :]).then_inc(s_out, 16)
                sp.dma_start(out[(BLOCKS - 1) * P:N_NODES, :], enh[0:LAST, BLOCKS - 1, :]).then_inc(s_out, 16)
                sp.wait_ge(s_out, 48)

            @block.gpsimd
            def _(pool):
                nc.gpsimd.memset(hT[64:65, :, :], 1.0).then_inc(s_h1, 1)
                pool.wait_ge(s_h1, 1)
                nc.gpsimd.tensor_tensor(x1b, x1[:, :, 0:H], bcv(1), ALU.add).then_inc(s_xb, 1)

            @block.tensor
            def _(pe):
                def mlp1(c):
                    b0, nb = CH[c]
                    if c >= 2:
                        pe.wait_ge(s_m1c, c - 1)
                    nc.tensor.matmul(bank(2 + c % 2)[0:64, 0:nb * P], w1s, x1T[:, b0:b0 + nb, :].rearrange("p b n -> p (b n)"),
                                     start=True, stop=True).then_inc(s_m1, 1)

                mlp1(0)
                pe.wait_ge(s_h1, 1)
                for c, (b0, nb) in enumerate(CH):
                    if c + 1 < len(CH):
                        mlp1(c + 1)
                    pe.wait_ge(s_m1c, c + 1)
                    if c >= 2:
                        pe.wait_ge(s_m2c, c - 1)
                    for k in range(nb):
                        dest = bank(4 + c % 2)[:, k * P:(k + 1) * P]
                        last = nc.tensor.matmul(dest, hT[0:65, c % 2, k * P:(k + 1) * P], w2s[0:65, :], start=True, stop=True)
                    last.then_inc(s_m2, 1)

            @block.scalar
            def _(act):
                def relu(c):
                    nb = CH[c][1]
                    act.wait_ge(s_m1, c + 1)
                    if c >= 2:
                        act.wait_ge(s_m2, c - 1)
                    nc.scalar.activation(hT[0:64, c % 2, 0:nb * P], bank(2 + c % 2)[0:64, 0:nb * P], ACT.Relu, bias=b1s[0:64, :]).then_inc(s_m1c, 1)

                relu(0)
                for c, (b0, nb) in enumerate(CH):
                    if c + 1 < len(CH):
                        relu(c + 1)
                    if c == 6:
                        squares.make(agg1[:, :, 0:H], agg1[:, :, 0:H])
                    act.wait_ge(s_m2, c + 1)
                    nc.scalar.activation(enh[:, b0:b0 + nb, :].rearrange("p b n -> p (b n)"), bank(4 + c % 2)[:, 0:nb * P], ACT.Copy).then_inc(s_m2c, 1)
                dist = red[:, 3, :]
                act.wait_ge(s_fq, 1)
                nc.scalar.activation(dist, dist, ACT.Sqrt).then_inc(s_fc2, 1)
                act.wait_ge(s_fc2, 1)
                nc.scalar.activation(dist, dist, ACT.Tanh).then_inc(s_fq, 1)
                squares.make(enh, x_sb[:])
                act.wait_ge(s_fq, 3)
                nc.scalar.activation(red[:, 1, :], red[:, 1, :], ACT.Sqrt).then_inc(s_fc2, 1)
                squares.make(enh, x_sb[:])
                act.wait_ge(s_fq, 4)
                nc.scalar.activation(red[:, 1, :], red[:, 1, :], ACT.Sqrt).then_inc(s_fc2, 1)

            @block.vector
            def _(dve):
                n = [0]

                def after(ins):
                    n[0] += 1
                    ins.then_inc(s_f, 1)
                    dve.wait_ge(s_f, n[0])

                roots = [1]

                def root():
                    dve.sem_inc(s_fq, 1)
                    roots[0] += 1
                    dve.wait_ge(s_fc2, roots[0])

                sm = agg1
                cntv = red[:, 4, :]
                after(nc.vector.tensor_scalar(cntv, sm[:, :, H:H + 1].rearrange("p b a -> p (b a)"), 1.0, None, ALU.max))
                after(nc.vector.reciprocal(cntv, cntv))
                after(nc.vector.tensor_tensor(sm[:, :, 0:H], sm[:, :, 0:H], bc(cntv), ALU.mult))
                for part in PARTS:
                    squares.ask(nc.vector.tensor_tensor(sm[:, part, 0:H], x1[:, part, 0:H], sm[:, part, 0:H], ALU.subtract))
                for part in PARTS:
                    squares.wait()
                    last = nc.vector.tensor_reduce(red[:, 3, part], sm[:, part, 0:H], op=ALU.add, axis=AX_X)
                after(last)
                dve.sem_inc(s_fq, 1)
                dve.wait_ge(s_m2c, len(CH))
                dve.wait_ge(s_fq, 2)
                after(nc.vector.tensor_scalar(red[:, 3, :], red[:, 3, :], ALPHA, None, ALU.mult))
                after(nc.vector.tensor_tensor(enh, enh, bc(red[:, 3, :]), ALU.mult))
                after(nc.vector.tensor_tensor(enh, enh, x1[:, :, 0:H], ALU.add))
                layernorm(after, squares, root, enh, x_sb[:], enh)
                after(nc.vector.tensor_tensor(enh, enh, bcv(0), ALU.mult))
                dve.wait_ge(s_xb, 1)
                after(nc.vector.tensor_tensor(enh, enh, x1b, ALU.add))
                layernorm(after, squares, root, enh, x_sb[:], enh, s_yw)



_INS = ["x", "src", "dst", "edge_attr_128", "L0_gnn_W", "L0_gnn_b", "L0_gnn_gamma", "L0_gnn_beta",
        "L1_gnn_W1", "L1_gnn_b1", "L1_gnn_W2", "L1_gnn_b2", "L1_gnn_gamma", "L1_gnn_beta"]


def kernel(**inputs):
    import numpy as _np
    import concourse.bacc as _bacc
    from concourse import mybir as _mybir
    from concourse.bass_utils import run_bass_kernel_spmd as _run

    nc = _bacc.Bacc("TRN2", target_bir_lowering=False, num_devices=1)
    arrays, args = {}, []
    for name in _INS:
        a = _np.ascontiguousarray(inputs[name])
        arrays[f"in_{name}"] = a
        args.append(nc.dram_tensor(f"in_{name}", a.shape, _mybir.dt.from_np(a.dtype), kind="ExternalInput").ap())
    args.append(nc.dram_tensor("out_0", (N_NODES, H), _mybir.dt.float32, kind="ExternalOutput").ap())
    build(nc, *args)
    r = _run(nc, [arrays], core_ids=[0])
    return r.results[0]["out_0"]
```
